# Optimizing a Trainium2 kernel written in Bass

```python
import numpy as np
import jax
import jax.numpy as jnp

def _softmax(x, axis=-1):
    return jax.nn.softmax(x, axis=axis)
def _gelu(x):
    return jax.nn.gelu(x, approximate=True)
def _silu(x):
    return jax.nn.silu(x)
def _sigmoid(x):
    return jax.nn.sigmoid(x)
def _layernorm(x, axis=-1, eps=1e-5):
    m = jnp.mean(x, axis=axis, keepdims=True)
    v = jnp.var(x, axis=axis, keepdims=True)
    return (x - m) / jnp.sqrt(v + eps)
def _scatter_add(tgt, idx, src, axis=0):
    return tgt.at[idx].add(src)
def _segment_sum(src, seg, n):
    return jax.ops.segment_sum(src, seg, n)

kernel_name = 'mk_conv_preact_d1_conv_nchw512_085b81'

def setup_inputs(seed: int = 0):
    np.random.seed(seed)
    _w = jnp.asarray
    def _rec_inputs():
        import jax
        import jax.numpy as jnp
        _gk = jax.random.key(seed)
        x = -0.000125 + 0.9999 * jax.random.normal(jax.random.fold_in(_gk, 1), (4, 512, 128, 128), jnp.float32)
        return x
    x = _rec_inputs()
    def _L0_conv_setup():
        import jax, jax.numpy as jnp
        import numpy as np
        B, C, H, W = (4, 512, 128, 128)
        CQK = C // 8

        def _criss_cross(q, k, v):
            _, _, h, w = q.shape
            e_row = jnp.einsum('bchw,bchi->bihw', q, k)
            e_col = jnp.einsum('bchw,bcjw->bjhw', q, k)
            diag = jnp.eye(h, dtype=bool)[None, :, :, None]
            e_col = jnp.where(diag, -jnp.inf, e_col)
            attn = jax.nn.softmax(jnp.concatenate([e_row, e_col], axis=1), axis=1)
            a_row, a_col = (attn[:, :w], attn[:, w:])
            out = jnp.einsum('bihw,bchi->bchw', a_row, v) + jnp.einsum('bjhw,bcjw->bchw', a_col, v)
            return out
        key = jax.random.key(seed)
        ks = jax.random.split(key, 4)

        def w(k, shape, fan_in):
            return jax.random.normal(k, shape, jnp.float32) * np.float32(1.0 / np.sqrt(fan_in))
        return {'x': jax.random.normal(ks[0], (B, C, H, W), jnp.float32), 'Wq': w(ks[1], (CQK, C), C), 'bq': jnp.zeros((CQK,), jnp.float32), 'Wk': w(ks[2], (CQK, C), C), 'bk': jnp.zeros((CQK,), jnp.float32), 'Wv': w(ks[3], (C, C), C), 'bv': jnp.zeros((C,), jnp.float32)}
    _L0_conv_all = _L0_conv_setup()
    _L0_conv_in = {k: v for k, v in _L0_conv_all.items() if k in ('Wq', 'bq', 'Wk', 'bk', 'Wv', 'bv', )}
    del _L0_conv_all

    return {
        "x": x,
        "L0_conv_Wq": _L0_conv_in["Wq"],
        "L0_conv_bq": _L0_conv_in["bq"],
        "L0_conv_Wk": _L0_conv_in["Wk"],
        "L0_conv_bk": _L0_conv_in["bk"],
        "L0_conv_Wv": _L0_conv_in["Wv"],
        "L0_conv_bv": _L0_conv_in["bv"],
    }

def reference(x, L0_conv_Wq, L0_conv_bq, L0_conv_Wk, L0_conv_bk, L0_conv_Wv, L0_conv_bv):
    import jax
    import jax.numpy as jnp
    def _L0_conv_ref(x, Wq, bq, Wk, bk, Wv, bv):
        import jax, jax.numpy as jnp
        import numpy as np
        B, C, H, W = (4, 512, 128, 128)
        CQK = C // 8

        def _criss_cross(q, k, v):
            _, _, h, w = q.shape
            e_row = jnp.einsum('bchw,bchi->bihw', q, k)
            e_col = jnp.einsum('bchw,bcjw->bjhw', q, k)
            diag = jnp.eye(h, dtype=bool)[None, :, :, None]
            e_col = jnp.where(diag, -jnp.inf, e_col)
            attn = jax.nn.softmax(jnp.concatenate([e_row, e_col], axis=1), axis=1)
            a_row, a_col = (attn[:, :w], attn[:, w:])
            out = jnp.einsum('bihw,bchi->bchw', a_row, v) + jnp.einsum('bjhw,bcjw->bchw', a_col, v)
            return out
        proj = lambda Wm, bm: jnp.einsum('bchw,oc->bohw', x, Wm) + bm[None, :, None, None]
        q = proj(Wq, bq)
        k = proj(Wk, bk)
        v = proj(Wv, bv)
        return _criss_cross(q, k, v)

    def _gn(v, G=32, eps=1e-5):
        B_, C_, H_, W_ = v.shape
        g = v.reshape(B_, G, C_ // G, H_, W_)
        m = jnp.mean(g, axis=(2, 3, 4), keepdims=True)
        s = jnp.var(g, axis=(2, 3, 4), keepdims=True)
        return ((g - m) / jnp.sqrt(s + eps)).reshape(v.shape)

    def _ln_c(v, eps=1e-6):
        m = jnp.mean(v, axis=1, keepdims=True)
        s = jnp.var(v, axis=1, keepdims=True)
        return (v - m) / jnp.sqrt(s + eps)

    def _ln_t(v, eps=1e-5):
        m = jnp.mean(v, axis=-1, keepdims=True)
        s = jnp.var(v, axis=-1, keepdims=True)
        return (v - m) / jnp.sqrt(s + eps)

    def _to_tokens(v):
        B_, C_, H_, W_ = v.shape
        return v.reshape(B_, C_, H_ * W_).transpose(0, 2, 1)
    def _from_tokens(t, like):
        B_, C_, H_, W_ = like.shape
        return t.transpose(0, 2, 1).reshape(B_, C_, H_, W_)

    x = x + _L0_conv_ref(_gn(x), L0_conv_Wq, L0_conv_bq, L0_conv_Wk, L0_conv_bk, L0_conv_Wv, L0_conv_bv)
    return x


_drawn_inputs = setup_inputs


def setup_inputs(seed=0):
    import zlib

    import numpy as np

    out = dict(_drawn_inputs(seed))
    spreads = {'L0_conv_bq': (0.0, 0.1), 'L0_conv_bk': (0.0, 0.1), 'L0_conv_bv': (0.0, 0.1)}
    factors = {}
    for name, (base, spread) in spreads.items():
        noise = np.random.default_rng([zlib.crc32(name.encode()), seed]).standard_normal(out[name].shape)
        drawn = base * np.exp(spread * noise) if base else spread * noise
        out[name] = jnp.asarray(drawn.astype(out[name].dtype))
    for name, factor in factors.items():
        out[name] = (out[name] * factor).astype(out[name].dtype)
    return out
```

```python
from contextlib import ExitStack
from math import log

import concourse.bass as bass
from concourse import mybir

F32 = mybir.dt.float32
F16 = mybir.dt.float16
BF16 = mybir.dt.bfloat16
ALU = mybir.AluOpType
ACT = mybir.ActivationFunctionType
AXX = mybir.AxisListType.X

P = 128
EPS = 1e-5
X_SCALE = 2.0 ** 5
W_SCALE = 2.0 ** 8
P_SCALE_LOG2 = 12
PROJ_DOWN = 1.0 / (X_SCALE * W_SCALE)
ATT_DOWN = 2.0 ** -P_SCALE_LOG2
FAR = -3.0e38


def criss_cross_program(nc, x, wv_t, wqk_t, bqk, bv, ident, group_mean, onehot, far_diag, out):
    NB, C, H, W = x.shape
    KC = C // P
    CQ = wqk_t.shape[1] // 2
    assert H == P and W == P and 2 * CQ == P
    R = 4
    NG = H // R
    NI = NG // 2
    S = 4
    NT = H // (R * S)
    NS = 2
    PIX = R * W
    PIECES = 8
    PH = H // PIECES
    UR = 8
    BLK = 32
    MOVE = 3 * 16

    ctx = ExitStack()
    with ctx:
        def sb(name, shape, dt):
            return ctx.enter_context(nc.sbuf_tensor(name, shape, dt))

        def sem(name):
            return ctx.enter_context(nc.semaphore(name))

        v_dram = nc.dram_tensor("v_scratch", [H, W, KC * 2 * P], F16).ap()
        WLEN = 2 * KC * C + 2 * KC * P
        w_dram = nc.dram_tensor("w_scratch", [P, WLEN], F16).ap()

        region_a = sb("region_a", [P, H * 2 * W], F16)
        region_b = sb("region_b", [P, H * 2 * W], F16)
        region_c = sb("region_c", [P, H * W], F32)
        region_w = sb("region_w", [P, WLEN], F16)
        ident_f = sb("ident_f", [P, P], F32)
        group_f = sb("group_f", [P, P], F32)
        ident_b = sb("ident_b", [P, P], BF16)
        far_b = sb("far_b", [P, P], BF16)
        onehot_b = sb("onehot_b", [P, BLK], BF16)
        bqk_s = sb("bqk_s", [P, 1], F32)
        bv_s = sb("bv_s", [P, KC], F32)
        bv_now = sb("bv_now", [P, 1], F32)
        norm_scale = sb("norm_scale", [P, KC], F32)
        norm_bias = sb("norm_bias", [P, KC], F32)
        small = sb("small", [P, 12, KC], F32)

        qk_rows = region_a[:].rearrange("p (h t w) -> p h t w", h=H, t=2)
        q_pair, k_high = qk_rows[:, :, 0, :], qk_rows[:, :, 1, :]
        prob_row = qk_rows
        prob_col = region_b[:].rearrange("p (w t h) -> p w t h", w=W, t=2)
        acc = region_c[:].rearrange("p (h w) -> p h w", h=H)
        c16 = region_c[:].bitcast(F16)
        k_low = c16[:, 0:H * W].rearrange("p (h w) -> p h w", h=H)

        XT = 2 * KC * PIX
        b32 = region_b[:].bitcast(F32)
        x_tile = [b32[:, s * KC * PIX:(s + 1) * KC * PIX].rearrange("p (k n) -> p k n", k=KC) for s in range(NS)]
        o = NS * XT
        x_high = [region_b[:, o + s * XT:o + s * XT + KC * PIX].rearrange("p (k n) -> p k n", k=KC) for s in range(NS)]
        x_low = [region_b[:, o + s * XT + KC * PIX:o + (s + 1) * XT].rearrange("p (k n) -> p k n", k=KC)
                 for s in range(NS)]
        o += NS * XT
        v_tile = [region_b[:, o + s * XT:o + (s + 1) * XT].rearrange("p (r k t c) -> p r k t c", r=R, k=KC, t=2)
                  for s in range(NS)]
        o += NS * XT
        stat_tile = [region_b[:, o + s * XT:o + (s + 1) * XT].bitcast(F32).rearrange("p (k n) -> p k n", k=KC)
                     for s in range(NS)]

        at = [H * W // 2]

        def carve(n):
            at[0] += n
            return region_c[:, at[0] - n:at[0]]

        qk_wide = carve(PIX)
        q_low_stage = [carve(PIX // 2).bitcast(F16) for _ in range(NS)]
        bn = carve(KC * NG * 6).rearrange("p (k g s) -> p k g s", k=KC, g=NG)
        p_wide = [carve(UR * P) for _ in range(NS)]
        exp_junk = [p_wide[q // UR][:, (q % UR) * P:(q % UR + 1) * P] for q in range(S * R)]
        mx = [carve(P), carve(P)]
        zs = [carve(P), carve(P)]
        neg_max = carve(S * R)
        m_all = carve(P)
        shift2 = carve(2 * P)
        grown = carve(2 * P)
        z_all = carve(P)
        log_z = carve(P)
        neg_l = [carve(P), carve(P)]
        rest = carve(P)
        neg_l3 = [carve(3 * P // 2).bitcast(BF16).rearrange("p (t n) -> p t n", t=3) for _ in range(2)]
        l_stack = [carve(2 * P).bitcast(BF16).rearrange("p (b n) -> p b n", b=H // BLK) for _ in range(2)]
        assert at[0] <= H * W

        wv_high = region_w[:, 0:KC * C].rearrange("p (k n) -> p k n", k=KC)
        wv_low = region_w[:, KC * C:2 * KC * C].rearrange("p (k n) -> p k n", k=KC)
        o = 2 * KC * C
        wqk_high = region_w[:, o:o + KC * P].rearrange("p (k n) -> p k n", k=KC)
        wqk_low = region_w[:, o + KC * P:o + 2 * KC * P].rearrange("p (k n) -> p k n", k=KC)
        VT = R * 2 * P
        v_ring = [region_w[:, s * VT:(s + 1) * VT].rearrange("p (r t c) -> p r t c", r=R, t=2) for s in range(S)]

        bank4 = ctx.enter_context(nc.psum_tensor("bank4", [P, S, 512], F32))
        bank_qk = ctx.enter_context(nc.psum_tensor("bank_qk", [P, 512], F32))
        bank_s = ctx.enter_context(nc.psum_tensor("bank_s", [P, 512], F32))

        const_in = sem("const_in")
        w_split = sem("w_split")
        w_stored = sem("w_stored")
        w_in = sem("w_in")
        x_in = [sem(f"x_in{s}") for s in range(NS)]
        stat_in = [sem(f"stat_in{s}") for s in range(NS)]
        stat_free = [sem(f"stat_free{s}") for s in range(NS)]
        stat_dve = sem("stat_dve")
        stat_pe = sem("stat_pe")
        stat_act = sem("stat_act")
        pool_chain = sem("pool_chain")
        parts_ready = [sem(f"parts_ready{s}") for s in range(NS)]
        qk_done = sem("qk_done")
        qk_wide_ready = sem("qk_wide_ready")
        qk_split = sem("qk_split")
        qh_ready = sem("qh_ready")
        qk_moved = [sem(f"qk_moved{s}") for s in range(NS)]
        v_done = sem("v_done")
        vh_ready = sem("vh_ready")
        v_stored = [sem(f"v_stored{s}") for s in range(NS)]
        bank_free = [sem(f"bank_free{s}") for s in range(S)]
        score_done = sem("score_done")
        max_ready = sem("max_ready")
        negmax_ready = sem("negmax_ready")
        expsum_done = sem("expsum_done")
        join_dve = sem("join_dve")
        join_pe = sem("join_pe")
        join_act = sem("join_act")
        stack_in = sem("stack_in")
        logit_done = sem("logit_done")
        exp_done = [sem(f"exp_done{s}") for s in range(NS)]
        ph_ready = sem("ph_ready")
        p_free = [sem(f"p_free{s}") for s in range(NS)]
        v_in = [sem(f"v_in{s}") for s in range(S)]
        att_done = [sem(f"att_done{s}") for s in range(S)]
        acc_in = [sem(f"acc_in{j}") for j in range(PIECES)]
        bias_set = sem("bias_set")
        pace = {e: sem(f"pace_{e}") for e in ("sp", "pool", "dve", "pe")}
        acc_ready = sem("acc_ready")
        acc_out = [sem(f"acc_out{j}") for j in range(PIECES)]

        CONSTS = 9 * 16
        JOIN_DVE, JOIN_PE, JOIN_ACT = 19, 2, 2
        STAT_DVE, STAT_PE = 14, 2
        V_AHEAD = NS * R
        BANK_PROJ, BANK_SCORE, BANK_ATT = NG, 2 * NT, KC * 2 * NT
        BANK_ALL = BANK_PROJ + BANK_SCORE + BANK_ATT

        x_pix = x.rearrange("b (k p) h w -> b p k (h w)", p=P)
        x_chunk = x.rearrange("b (k p) h w -> b k p h w", p=P)
        out_chunk = out.rearrange("b (k p) h w -> b k p h w", p=P)

        def per_image(eng, body):
            if NB > 1:
                with eng.Fori(0, NB - 1) as b:
                    body(b, True)
            body(NB - 1, False)

        def stand(eng, name):
            eng.sem_inc(pace[name], 1)

        block = ctx.enter_context(nc.Block())

        @block.sync
        def _(sp):
            sp.dma_start(b32[:, 0:KC * C].rearrange("p (k n) -> p k n", k=KC),
                         wv_t.rearrange("(k p) n -> p k n", p=P)).then_inc(const_in, 16)
            sp.dma_start(b32[:, KC * C:KC * C + KC * P].rearrange("p (k n) -> p k n", k=KC),
                         wqk_t.rearrange("(k p) n -> p k n", p=P)).then_inc(const_in, 16)
            t = KC * C + KC * P
            sp.dma_start(ident_f[:], ident).then_inc(const_in, 16)
            sp.dma_start(group_f[:], group_mean).then_inc(const_in, 16)
            sp.dma_start(b32[:, t:t + P], far_diag).then_inc(const_in, 16)
            sp.dma_start(b32[:, t + P:t + P + BLK], onehot).then_inc(const_in, 16)
            sp.dma_start(bqk_s[:], bqk.rearrange("(p a) -> p a", a=1)).then_inc(const_in, 16)
            sp.dma_start(bv_s[:], bv).then_inc(const_in, 16)
            sp.dma_start(b32[:, t + P + BLK:t + P + BLK + P], ident).then_inc(const_in, 16)
            sp.wait_ge(w_split, 3)
            sp.dma_start(w_dram, region_w[:]).then_inc(w_stored, 16)
            sp.wait_ge(w_stored, 16)

            def stat_load(b, i, s):
                sp.wait_ge(stat_free[s], b * NI + i + 1)
                sp.dma_start(stat_tile[s], x_pix[b][:, :, bass.ds((i * NS + s) * PIX, PIX)]
                             ).then_inc(stat_in[s], 16)

            with sp.Fori(0, NI) as i:
                for s in range(NS):
                    stat_load(0, i, s)

            def image(b, more):
                for s in range(S):
                    sp.wait_ge(att_done[s], b * KC * 2 * NT + 1)
                stand(sp, "sp")
                sp.dma_start(region_w[:], w_dram).then_inc(w_in, 16)
                with sp.Fori(0, NI) as i:
                    for s in range(NS):
                        sp.wait_ge(parts_ready[s], b * NI + i + 1)
                        sp.dma_start(x_tile[s], x_pix[b][:, :, bass.ds((i * NS + s) * PIX, PIX)]
                                     ).then_inc(x_in[s], 16)
                        if more:
                            stat_load(b + 1, i, s)
                for d in range(2):
                    sp.wait_ge(join_dve, b * JOIN_DVE + (13 if d == 0 else 19))
                    for part in range(3):
                        for k in range(H // BLK):
                            sp.dma_start(l_stack[d][part * BLK:(part + 1) * BLK, k, :],
                                         neg_l3[d][k * BLK:(k + 1) * BLK, part, :]).then_inc(stack_in, 16)
                for s in range(NS):
                    sp.wait_ge(v_stored[s], 16 * NI * (b + 1) + 16)
                stand(sp, "sp")
                with sp.Fori(0, KC) as c:
                    for d in range(2):
                        src = v_dram.rearrange("h w c -> w h c") if d == 0 else v_dram
                        with sp.Fori(0, NT) as i:
                            n = ((b * KC + c) * 2 + d) * NT + i
                            for s in range(S):
                                sp.wait_ge(att_done[s], n + 1)
                                sp.dma_start(v_ring[s].rearrange("p r t c -> p r (t c)"),
                                             src[:, bass.ds((i * S + s) * R, R), bass.ds(c * 2 * P, 2 * P)]
                                             ).then_inc(v_in[s], 16)

            per_image(sp, image)

        @block.gpsimd
        def _(pool):
            def image(b, more):
                pool.wait_ge(stat_dve, (b + 1) * STAT_DVE)
                stand(pool, "pool")
                with pool.Fori(0, NI) as i:
                    n = b * NI + i
                    for s in range(NS):
                        base = (n * NS + s) * (KC + 1)
                        pool.wait_ge(x_in[s], 16 * n + 16)
                        stand(pool, "pool")
                        for k in range(KC):
                            nc.gpsimd.tensor_scalar(x_tile[s][:, k], x_tile[s][:, k], norm_scale[:, k:k + 1],
                                                    norm_bias[:, k:k + 1], ALU.mult, ALU.add).then_inc(pool_chain, 1)
                        pool.wait_ge(pool_chain, base + KC)
                        pool.wait_ge(v_done, (n * NS + s) * R + R)
                        stand(pool, "pool")
                        nc.gpsimd.tensor_copy(x_high[s], x_tile[s]).then_inc(pool_chain, 1)
                        pool.wait_ge(pool_chain, base + KC + 1)
                        nc.gpsimd.tensor_tensor(x_low[s], x_tile[s], x_high[s], ALU.subtract
                                                ).then_inc(parts_ready[s], 1)

            for s in range(NS):
                pool.sem_inc(parts_ready[s], 1)
            per_image(pool, image)

        @block.tensor
        def _(pe):
            for s in range(NS):
                pe.sem_inc(exp_done[s], 1)
            pe.sem_inc(v_done, V_AHEAD)
            for s in range(S):
                pe.sem_inc(att_done[s], 1)
                pe.sem_inc(bank_free[s], 1)

            def three(dst, left, right, n_k):
                for k in range(n_k):
                    pe.matmul(dst, left[0](k), right[0](k), start=(k == 0), stop=False)
                    pe.matmul(dst, left[0](k), right[1](k), start=False, stop=False)
                    last = pe.matmul(dst, left[1](k), right[0](k), start=False, stop=(k == n_k - 1))
                return last

            def statistics(b):
                pe.wait_ge(stat_dve, b * STAT_DVE + 2)
                pe.matmul(bank_s[:, 0:KC], group_f[:], small[:, 0, :], start=True, stop=True).then_inc(stat_pe, 1)
                pe.wait_ge(stat_dve, b * STAT_DVE + 6)
                pe.matmul(bank_s[:, KC:2 * KC], group_f[:], small[:, 4, :], start=True, stop=True
                          ).then_inc(stat_pe, 1)

            def image(b, more):
                pe.wait_ge(w_in, 16 * b + 16)
                stand(pe, "pe")
                with pe.Fori(0, NI) as i:
                    n = b * NI + i
                    for s in range(NS):
                        g = n * NS + s
                        pe.wait_ge(parts_ready[s], n + 2)
                        pe.wait_ge(qk_wide_ready, g + 1)
                        three(bank_qk[:], (lambda k: wqk_high[:, k], lambda k: wqk_low[:, k]),
                              (lambda k: x_high[s][:, k], lambda k: x_low[s][:, k]), KC).then_inc(qk_done, 1)
                        for r in range(R):
                            px = slice(r * W, (r + 1) * W)
                            pe.wait_ge(bank_free[r], b * BANK_ALL + i * NS + s + 1)
                            last = three(bank4[:, r], (lambda k: x_high[s][:, k, px], lambda k: x_low[s][:, k, px]),
                                         (lambda k: wv_high[:, k], lambda k: wv_low[:, k]), KC)
                            last.then_inc(v_done, 1)
                if more:
                    statistics(b + 1)

                for s in range(NS):
                    pe.wait_ge(qk_moved[s], MOVE * NI * (b + 1) + MOVE)
                stand(pe, "pe")
                for d in range(2):
                    with pe.Fori(0, NT) as i:
                        for s in range(S):
                            pe.wait_ge(bank_free[s], b * BANK_ALL + BANK_PROJ + d * NT + i + 1)
                            for r in range(R):
                                at = (i * S + s) * R + r
                                dst = bank4[:, s, r * P:(r + 1) * P]
                                q, kh, kl = ((q_pair, k_high, k_low) if d == 0 else
                                             [t.rearrange("p h w -> p w h") for t in (q_pair, k_high, k_low)])
                                line = bass.ds(at, 1)
                                qs = q[:, line, :].rearrange("p a n -> p (a n)")
                                pe.matmul(dst, qs, kh[:, line, :].rearrange("p a n -> p (a n)"),
                                          start=True, stop=False)
                                last = pe.matmul(dst, qs, kl[:, line, :].rearrange("p a n -> p (a n)"),
                                                 start=False, stop=(d == 0))
                                if d == 1:
                                    last = pe.matmul(dst, ident_b[:], far_b[:], start=False, stop=True)
                            last.then_inc(score_done, 1)

                for s in range(S):
                    pe.wait_ge(bank_free[s], b * BANK_ALL + BANK_PROJ + BANK_SCORE + 1)
                pe.transpose(bank_s[:, 0:P], mx[0], ident_f[:])
                pe.transpose(bank_s[:, P:2 * P], zs[0], ident_f[:]).then_inc(join_pe, 1)
                pe.wait_ge(join_dve, b * JOIN_DVE + 8)
                pe.transpose(bank_s[:, 2 * P:3 * P], neg_l[0], ident_f[:]).then_inc(join_pe, 1)

                for s in range(S):
                    pe.wait_ge(bank_free[s], b * BANK_ALL + BANK_PROJ + BANK_SCORE + 1)
                pe.wait_ge(stack_in, (b + 1) * 2 * 3 * (H // BLK) * 16)
                stand(pe, "pe")
                for d in (1, 0):
                    q, kh, kl = ((q_pair, k_high, k_low) if d == 0 else
                                 [t.rearrange("p h w -> p w h") for t in (q_pair, k_high, k_low)])
                    with pe.Fori(0, H // BLK) as blk:
                        shifts = l_stack[d][0:3 * BLK, bass.ds(blk, 1), :].rearrange("p a n -> p (a n)")
                        for u in range(BLK // UR):
                            s = u % NS
                            pe.wait_ge(exp_done[s],
                                       ((b * 2 + (1 - d)) * (H // BLK) + blk) * (BLK // UR // NS) + u // NS + 1)
                            for r in range(UR):
                                line = bass.ds(blk * BLK + u * UR + r, 1)
                                dst = bank4[:, s * 2 + r // R, (r % R) * P:(r % R + 1) * P]
                                hot = onehot_b[0:3 * BLK, u * UR + r:u * UR + r + 1].to_broadcast([3 * BLK, P])
                                qs = q[:, line, :].rearrange("p a n -> p (a n)")
                                pe.matmul(dst, kh[:, line, :].rearrange("p a n -> p (a n)"), qs,
                                          start=True, stop=False)
                                pe.matmul(dst, kl[:, line, :].rearrange("p a n -> p (a n)"), qs,
                                          start=False, stop=False)
                                if d == 1:
                                    pe.matmul(dst, ident_b[:], far_b[:], start=False, stop=False)
                                last = pe.matmul(dst, hot, shifts, start=False, stop=True)
                            last.then_inc(logit_done, 1)

                for s in range(NS):
                    pe.wait_ge(p_free[s], (b + 1) * 2 * (H // UR // NS) + 1)
                stand(pe, "pe")
                with pe.Fori(0, KC) as c:
                    for d in range(2):
                        probs = prob_row if d == 0 else prob_col
                        with pe.Fori(0, NT) as i:
                            m = (c * 2 + d) * NT + i
                            n = b * KC * 2 * NT + m
                            for s in range(S):
                                pe.wait_ge(v_in[s], 16 * n + 16)
                                pe.wait_ge(bank_free[s], b * BANK_ALL + BANK_PROJ + BANK_SCORE + m + 1)
                                for r in range(R):
                                    line = bass.ds((i * S + s) * R + r, 1)
                                    ph = probs[:, line, 0, :].rearrange("p a n -> p (a n)")
                                    pl = probs[:, line, 1, :].rearrange("p a n -> p (a n)")
                                    last = three(bank4[:, s, r * P:(r + 1) * P],
                                                 (lambda k: v_ring[s][:, r, 0], lambda k: v_ring[s][:, r, 1]),
                                                 (lambda k: ph, lambda k: pl), 1)
                                last.then_inc(att_done[s], 1)
            statistics(0)
            pe.sem_inc(qk_wide_ready, 1)
            per_image(pe, image)

        @block.scalar
        def _(act):
            for s in range(NS):
                act.sem_inc(v_stored[s], 16)
                act.sem_inc(p_free[s], 1)
            for j in range(PIECES):
                act.sem_inc(acc_out[j], 16)

            def statistics(b):
                act.wait_ge(stat_dve, b * STAT_DVE + 7)
                nc.scalar.activation(small[:, 6, :], small[:, 5, :], ACT.Sqrt).then_inc(stat_act, 1)

            def image(b, more):
                for j in range(PIECES):
                    act.wait_ge(acc_out[j], 16 * b * KC + 16)
                with act.Fori(0, NI) as i:
                    n = b * NI + i
                    for s in range(NS):
                        g = n * NS + s
                        act.wait_ge(qk_done, g + 1)
                        nc.scalar.activation(qk_wide, bank_qk[:], ACT.Identity, bias=bqk_s[:, 0:1], scale=PROJ_DOWN
                                             ).then_inc(qk_wide_ready, 1)
                        act.wait_ge(v_stored[s], 16 * n + 16)
                        act.wait_ge(qk_split, g + 1)
                        rows = bass.ds((i * NS + s) * R, R)
                        act.dma_start(qk_rows[CQ:P, rows, 0, :],
                                      q_low_stage[s][0:CQ].rearrange("p (r w) -> p r w", r=R)
                                      ).then_inc(qk_moved[s], 16)
                        act.dma_start(qk_rows[0:CQ, rows, 1, :], qk_rows[CQ:P, rows, 1, :]).then_inc(qk_moved[s], 16)
                        act.dma_start(k_low[0:CQ, rows, :], k_low[CQ:P, rows, :]).then_inc(qk_moved[s], 16)
                        for r in range(R):
                            act.wait_ge(v_done, V_AHEAD + g * R + r + 1)
                            nc.scalar.activation(v_tile[s][:, r, :, 0, :],
                                                 bank4[:, r].rearrange("p (k c) -> p k c", k=KC),
                                                 ACT.Copy, scale=PROJ_DOWN).then_inc(vh_ready, 1)
                        for r in range(R):
                            act.wait_ge(bank_free[r], b * BANK_ALL + i * NS + s + 2)
                        act.dma_start(v_dram[bass.ds((i * NS + s) * R, R)].rearrange("r w c -> w r c"),
                                      v_tile[s].rearrange("p r k t c -> p r (k t c)")).then_inc(v_stored[s], 16)
                if more:
                    statistics(b + 1)

                for d in range(2):
                    with act.Fori(0, NT) as i:
                        n = (b * 2 + d) * NT + i
                        for s in range(S):
                            act.wait_ge(negmax_ready, n * S + s + 1)
                            for r in range(R):
                                q = s * R + r
                                ins = nc.scalar.activation(exp_junk[q], bank4[:, s, r * P:(r + 1) * P], ACT.Exp,
                                                           bias=neg_max[:, q:q + 1], accum_out=zs[d][:, bass.ds(i * S * R + q, 1)])
                            ins.then_inc(bank_free[s], 1)

                act.wait_ge(join_dve, b * JOIN_DVE + 3)
                nc.scalar.activation(grown, shift2, ACT.Exp).then_inc(join_act, 1)
                act.wait_ge(join_dve, b * JOIN_DVE + 6)
                nc.scalar.activation(log_z, z_all, ACT.Ln).then_inc(join_act, 1)

                for d in (1, 0):
                    with act.Fori(0, H // UR // NS) as i:
                        n = (b * 2 + (1 - d)) * (H // UR // NS) + i
                        for s in range(NS):
                            act.wait_ge(logit_done, n * NS + s + 1)
                            act.wait_ge(p_free[s], n + 1)
                            nc.scalar.activation(p_wide[s], bank4[:, 2 * s:2 * s + 2, :].rearrange("p a n -> p (a n)"),
                                                 ACT.Exp).then_inc(exp_done[s], 1)

                for s in range(NS):
                    act.wait_ge(p_free[s], (b + 1) * 2 * (H // UR // NS) + 1)
                with act.Fori(0, KC) as c:
                    n = b * KC + c
                    for j in range(PIECES):
                        act.wait_ge(acc_out[j], 16 * n + 16)
                        act.dma_start(acc[:, j * PH:(j + 1) * PH, :], x_chunk[b][c][:, j * PH:(j + 1) * PH, :]
                                      ).then_inc(acc_in[j], 16)
                    nc.scalar.activation(bv_now[:], bv_s[:, bass.ds(c, 1)], ACT.Copy).then_inc(bias_set, 1)
                    act.wait_ge(bias_set, n + 1)
                    for j in range(PIECES):
                        act.wait_ge(acc_in[j], 16 * n + 16)
                        nc.scalar.activation(acc[:, j * PH:(j + 1) * PH, :], acc[:, j * PH:(j + 1) * PH, :],
                                             ACT.Identity, bias=bv_now[:]).then_inc(acc_ready, 1)
                    for s in range(S):
                        act.wait_ge(bank_free[s], b * BANK_ALL + BANK_PROJ + BANK_SCORE + (c + 1) * 2 * NT + 1)
                    for j in range(PIECES):
                        act.dma_start(out_chunk[b][c][:, j * PH:(j + 1) * PH, :], acc[:, j * PH:(j + 1) * PH, :]
                                      ).then_inc(acc_out[j], 16)

            statistics(0)
            per_image(act, image)
            for j in range(PIECES):
                act.wait_ge(acc_out[j], 16 * NB * KC + 16)

        @block.vector
        def _(dve):
            for s in range(NS):
                dve.sem_inc(stat_free[s], 1)
                dve.sem_inc(qk_moved[s], MOVE)

            dve.wait_ge(const_in, CONSTS)
            wide = b32[:, 0:KC * C + KC * P]
            nc.vector.tensor_scalar(wide, wide, W_SCALE, None, ALU.mult).then_inc(w_split, 1)
            dve.wait_ge(w_split, 1)
            wv_wide, wqk_wide = b32[:, 0:KC * C], b32[:, KC * C:KC * C + KC * P]
            wvh, wvl = region_w[:, 0:KC * C], region_w[:, KC * C:2 * KC * C]
            o = 2 * KC * C
            wqh, wql = region_w[:, o:o + KC * P], region_w[:, o + KC * P:o + 2 * KC * P]
            t = KC * C + KC * P
            nc.vector.tensor_copy(far_b[:], b32[:, t:t + P])
            nc.vector.tensor_copy(onehot_b[:], b32[:, t + P:t + P + BLK])
            nc.vector.tensor_copy(ident_b[:], b32[:, t + P + BLK:t + P + BLK + P])
            nc.vector.tensor_copy(wvh, wv_wide)
            nc.vector.tensor_copy(wqh, wqk_wide).then_inc(w_split, 1)
            dve.wait_ge(w_split, 2)
            nc.vector.tensor_tensor(wvl, wv_wide, wvh, ALU.subtract)
            nc.vector.tensor_tensor(wql, wqk_wide, wqh, ALU.subtract).then_inc(w_split, 1)

            def stat_group(b, i, s):
                dve.wait_ge(stat_in[s], 16 * (b * NI + i) + 16)
                for k in range(KC):
                    last = nc.vector.bn_stats(bn[:, k, bass.ds(i * NS + s, 1), :].rearrange("p a s -> p (a s)"),
                                              stat_tile[s][:, k])
                last.then_inc(stat_free[s], 1)

            def statistics(b):
                count = [0]

                def link(ins):
                    ins.then_inc(stat_dve, 1)
                    count[0] += 1
                    dve.wait_ge(stat_dve, b * STAT_DVE + count[0])

                for s in range(NS):
                    dve.wait_ge(stat_free[s], (b + 1) * NI + 1)
                stand(dve, "dve")
                for k in range(KC):
                    last = nc.vector.bn_aggr(small[:, 8 + 0:10, :].rearrange("p a k -> p (a k)")[:, 2 * k:2 * k + 2],
                                             bn[:, k].rearrange("p g s -> p (g s)"))
                link(last)
                mv = small[:, 8:10, :].rearrange("p a k -> p (a k)").rearrange("p (k t) -> p t k", t=2)
                mean, mean_g, d, d2, mom, var_g, sd, y = (small[:, j, :] for j in range(8))
                link(nc.vector.tensor_copy(mean, mv[:, 0, :]))
                dve.wait_ge(stat_pe, STAT_PE * b + 1)
                link(nc.vector.tensor_copy(mean_g, bank_s[:, 0:KC]))
                link(nc.vector.tensor_tensor(d, mean, mean_g, ALU.subtract))
                link(nc.vector.tensor_tensor(d2, d, d, ALU.mult))
                link(nc.vector.tensor_tensor(mom, d2, mv[:, 1, :], ALU.add))
                dve.wait_ge(stat_pe, STAT_PE * b + 2)
                link(nc.vector.tensor_scalar(var_g, bank_s[:, KC:2 * KC], EPS, None, ALU.add))
                dve.wait_ge(stat_act, b + 1)
                link(nc.vector.reciprocal(y, sd))
                link(nc.vector.tensor_tensor(d, y, y, ALU.mult))
                link(nc.vector.tensor_tensor(d2, d, var_g, ALU.mult))
                link(nc.vector.tensor_scalar(d, d2, -0.5, 1.5, ALU.mult, ALU.add))
                link(nc.vector.tensor_tensor(d2, y, d, ALU.mult))
                link(nc.vector.tensor_scalar(norm_scale[:], d2, X_SCALE, None, ALU.mult))
                link(nc.vector.scalar_tensor_tensor(out=norm_bias[:], in0=mean_g, scalar=-1.0,
                                                    in1=norm_scale[:], op0=ALU.mult, op1=ALU.mult))
                stand(dve, "dve")
                assert count[0] == STAT_DVE

            def image(b, more):
                for j in range(PIECES):
                    dve.wait_ge(acc_out[j], 16 * b * KC + 16)
                stand(dve, "dve")
                with dve.Fori(0, NI) as i:
                    n = b * NI + i
                    for s in range(NS):
                        g = n * NS + s
                        rows = bass.ds((i * NS + s) * R, R)
                        wide_q = qk_wide[0:CQ].rearrange("p (r w) -> p r w", r=R)
                        wide_k = qk_wide[CQ:P].rearrange("p (r w) -> p r w", r=R)
                        dve.wait_ge(qk_moved[s], MOVE * n + MOVE)
                        dve.wait_ge(qk_wide_ready, g + 2)
                        nc.vector.tensor_copy(qk_rows[0:CQ, rows, 0, :], wide_q).then_inc(qh_ready, 1)
                        nc.vector.tensor_copy(qk_rows[CQ:P, rows, 1, :], wide_k).then_inc(qh_ready, 1)
                        dve.wait_ge(qh_ready, 2 * g + 2)
                        nc.vector.tensor_tensor(q_low_stage[s][0:CQ].rearrange("p (r w) -> p r w", r=R), wide_q,
                                                qk_rows[0:CQ, rows, 0, :], ALU.subtract)
                        nc.vector.tensor_tensor(k_low[CQ:P, rows, :], wide_k, qk_rows[CQ:P, rows, 1, :],
                                                ALU.subtract).then_inc(qk_split, 1)
                        for r in range(R):
                            dve.wait_ge(vh_ready, g * R + r + 1)
                            bank = bank4[:, r].rearrange("p (k c) -> p k c", k=KC)
                            nc.vector.scalar_tensor_tensor(out=v_tile[s][:, r, :, 1, :], in0=bank, scalar=PROJ_DOWN,
                                                           in1=v_tile[s][:, r, :, 0, :], op0=ALU.mult,
                                                           op1=ALU.subtract).then_inc(bank_free[r], 1)
                        if more:
                            stat_group(b + 1, i, s)
                if more:
                    statistics(b + 1)

                for d in range(2):
                    with dve.Fori(0, NT) as i:
                        n = (b * 2 + d) * NT + i
                        for s in range(S):
                            u = n * S + s
                            dve.wait_ge(score_done, u + 1)
                            at = bass.ds((i * S + s) * R, R)
                            nc.vector.tensor_reduce(mx[d][:, at], bank4[:, s].rearrange("p (r n) -> p r n", r=R),
                                                    AXX, ALU.max).then_inc(max_ready, 1)
                            dve.wait_ge(max_ready, u + 1)
                            dve.wait_ge(bank_free[s], b * BANK_ALL + BANK_PROJ + d * NT + i + 1)
                            nc.vector.tensor_scalar(neg_max[:, s * R:(s + 1) * R], mx[d][:, at], -1.0, None,
                                                    ALU.mult).then_inc(negmax_ready, 1)

                count = [0]

                def link(ins):
                    ins.then_inc(join_dve, 1)
                    count[0] += 1
                    dve.wait_ge(join_dve, b * JOIN_DVE + count[0])

                def split3(d):
                    link(nc.vector.tensor_copy(neg_l3[d][:, 0, :], neg_l[d]))
                    link(nc.vector.tensor_tensor(rest, neg_l[d], neg_l3[d][:, 0, :], ALU.subtract))
                    link(nc.vector.tensor_copy(neg_l3[d][:, 1, :], rest))
                    link(nc.vector.tensor_tensor(rest, rest, neg_l3[d][:, 1, :], ALU.subtract))
                    link(nc.vector.tensor_copy(neg_l3[d][:, 2, :], rest))

                dve.wait_ge(join_pe, b * JOIN_PE + 1)
                link(nc.vector.tensor_tensor(m_all, bank_s[:, 0:P], mx[1], ALU.max))
                link(nc.vector.tensor_tensor(shift2[:, 0:P], bank_s[:, 0:P], m_all, ALU.subtract))
                link(nc.vector.tensor_tensor(shift2[:, P:2 * P], mx[1], m_all, ALU.subtract))
                dve.wait_ge(join_act, b * JOIN_ACT + 1)
                link(nc.vector.tensor_tensor(z_all, bank_s[:, P:2 * P], grown[:, 0:P], ALU.mult))
                link(nc.vector.tensor_tensor(rest, zs[1], grown[:, P:2 * P], ALU.mult))
                link(nc.vector.tensor_tensor(z_all, z_all, rest, ALU.add))
                dve.wait_ge(join_act, b * JOIN_ACT + 2)
                link(nc.vector.tensor_tensor(rest, m_all, log_z, ALU.add))
                link(nc.vector.tensor_scalar(neg_l[0], rest, -1.0, P_SCALE_LOG2 * log(2.0),
                                             ALU.mult, ALU.add))
                split3(0)
                dve.wait_ge(join_pe, b * JOIN_PE + 2)
                link(nc.vector.tensor_copy(neg_l[1], bank_s[:, 2 * P:3 * P]))
                split3(1)
                assert count[0] == JOIN_DVE

                for s in range(NS):
                    dve.wait_ge(v_stored[s], 16 * NI * (b + 1) + 16)
                stand(dve, "dve")
                for d in (1, 0):
                    probs = prob_col if d == 1 else prob_row
                    with dve.Fori(0, H // UR // NS) as i:
                        n = (b * 2 + (1 - d)) * (H // UR // NS) + i
                        for s in range(NS):
                            u = n * NS + s
                            lines = bass.ds((i * NS + s) * UR, UR)
                            src = p_wide[s].rearrange("p (r n) -> p r n", r=UR)
                            dve.wait_ge(exp_done[s], n + 2)
                            nc.vector.tensor_copy(probs[:, lines, 0, :], src).then_inc(ph_ready, 1)
                            dve.wait_ge(ph_ready, u + 1)
                            nc.vector.tensor_tensor(probs[:, lines, 1, :], src, probs[:, lines, 0, :],
                                                    ALU.subtract).then_inc(p_free[s], 1)

                with dve.Fori(0, KC) as c:
                    for d in range(2):
                        if d == 1:
                            for s in range(S):
                                dve.wait_ge(bank_free[s], b * BANK_ALL + BANK_PROJ + BANK_SCORE + (c * 2 + 1) * NT + 1)
                            stand(dve, "dve")
                        with dve.Fori(0, NT) as i:
                            n = ((b * KC + c) * 2 + d) * NT + i
                            if d == 0:
                                dve.wait_ge(acc_ready, (b * KC + c) * NT + i + 1)
                            for s in range(S):
                                lines = bass.ds((i * S + s) * R, R)
                                dve.wait_ge(att_done[s], n + 2)
                                part = acc[:, lines, :] if d == 0 else acc[:, :, lines]
                                prod = bank4[:, s].rearrange("p (r n) -> p r n" if d == 0 else "p (r n) -> p n r", r=R)
                                nc.vector.scalar_tensor_tensor(out=part, in0=prod, scalar=ATT_DOWN, in1=part,
                                                               op0=ALU.mult, op1=ALU.add).then_inc(bank_free[s], 1)

            with dve.Fori(0, NI) as i:
                for s in range(NS):
                    stat_group(0, i, s)
            statistics(0)
            per_image(dve, image)


_OUT = "out_dram"


def kernel(x, L0_conv_Wq, L0_conv_bq, L0_conv_Wk, L0_conv_bk, L0_conv_Wv, L0_conv_bv):
    import numpy as np
    import concourse.bacc as bacc
    from concourse.bass_utils import run_bass_kernel_spmd

    G = 16
    B, C, H, W = x.shape
    rows = np.arange(128)
    arrays = {
        "x_dram": np.ascontiguousarray(x),
        "wv_t_dram": np.ascontiguousarray(np.asarray(L0_conv_Wv).T),
        "wqk_t_dram": np.ascontiguousarray(np.concatenate([L0_conv_Wq, L0_conv_Wk], 0).T),
        "bqk_dram": np.concatenate([L0_conv_bq, L0_conv_bk]),
        "bv_dram": np.ascontiguousarray(np.asarray(L0_conv_bv).reshape(C // 128, 128).T),
        "ident_dram": np.eye(128, dtype=np.float32),
        "group_mean_dram": (rows[:, None] // G == rows[None] // G).astype(np.float32) / np.float32(G),
        "onehot_dram": (rows[:, None] % 32 == np.arange(32)[None]).astype(np.float32),
        "far_diag_dram": np.where(np.eye(128, dtype=bool), np.float32(FAR), np.float32(0)).astype(np.float32),
    }
    nc = bacc.Bacc("TRN2", target_bir_lowering=False, num_devices=1)
    args = [nc.dram_tensor(n, a.shape, mybir.dt.from_np(a.dtype), kind="ExternalInput").ap()
            for n, a in arrays.items()]
    args.append(nc.dram_tensor(_OUT, (B, C, H, W), F32, kind="ExternalOutput").ap())
    criss_cross_program(nc, *args)
    r = run_bass_kernel_spmd(nc, [arrays], core_ids=[0])
    return r.results[0][_OUT]
```

```python
from contextlib import ExitStack
from math import log

import concourse.bass as bass
from concourse import mybir

F32 = mybir.dt.float32
F16 = mybir.dt.float16
BF16 = mybir.dt.bfloat16
ALU = mybir.AluOpType
ACT = mybir.ActivationFunctionType
AXX = mybir.AxisListType.X

P = 128
EPS = 1e-5
X_SCALE = 2.0 ** 5
W_SCALE = 2.0 ** 8
P_SCALE_LOG2 = 12
PROJ_DOWN = 1.0 / (X_SCALE * W_SCALE)
ATT_DOWN = 2.0 ** -P_SCALE_LOG2
FAR = -3.0e38


def criss_cross_program(nc, x, wv_t, wqk_t, bqk, bv, ident, group_mean, onehot, far_diag, out):
    NB, C, H, W = x.shape
    KC = C // P
    CQ = wqk_t.shape[1] // 2
    assert H == P and W == P and 2 * CQ == P
    R = 4
    NG = H // R
    NI = NG // 2
    S = 4
    NT = H // (R * S)
    NS = 2
    PIX = R * W
    NX = 3
    UR = 8
    BLK = 32
    MOVE = 3 * 16

    ctx = ExitStack()
    with ctx:
        def sb(name, shape, dt):
            return ctx.enter_context(nc.sbuf_tensor(name, shape, dt))

        def sem(name):
            return ctx.enter_context(nc.semaphore(name))

        v_dram = nc.dram_tensor("v_scratch", [H, W, KC * 2 * P], F16).ap()
        WLEN = 2 * KC * C + 2 * KC * P
        w_dram = nc.dram_tensor("w_scratch", [P, WLEN], F16).ap()

        l_dram = nc.dram_tensor("shift_scratch", [2, 3, H, W], BF16).ap()

        region_a = sb("region_a", [P, H * 2 * W], F16)
        region_b = sb("region_b", [P, H * 2 * W], F16)
        region_c = sb("region_c", [P, H * W], F32)
        region_w = sb("region_w", [P, WLEN], F16)
        ident_f = sb("ident_f", [P, P], F32)
        group_f = sb("group_f", [P, P], F32)
        ident_b = sb("ident_b", [P, P], BF16)
        far_b = sb("far_b", [P, P], BF16)
        onehot_b = sb("onehot_b", [P, BLK], BF16)
        vectors = sb("vectors", [P, 3 + 3 * KC], F32)
        bqk_s, scratch1, bv_now = (vectors[:, j:j + 1] for j in range(3))
        bv_s, norm_scale, norm_bias = (vectors[:, 3 + j * KC:3 + (j + 1) * KC] for j in range(3))
        res_tiles = sb("res_tiles", [P, (NX - 1) * PIX], F32)
        small = sb("small", [P, 12, KC], F32)

        qk_rows = region_a[:].rearrange("p (h t w) -> p h t w", h=H, t=2)
        q_pair, k_high = qk_rows[:, :, 0, :], qk_rows[:, :, 1, :]
        prob_row = qk_rows
        prob_col = region_b[:].rearrange("p (w t h) -> p w t h", w=W, t=2)
        acc = region_c[:].rearrange("p (h w) -> p h w", h=H)
        c16 = region_c[:].bitcast(F16)
        k_low = c16[:, 0:H * W].rearrange("p (h w) -> p h w", h=H)

        XT = 2 * KC * PIX
        b32 = region_b[:].bitcast(F32)
        x_tile = [b32[:, s * KC * PIX:(s + 1) * KC * PIX].rearrange("p (k n) -> p k n", k=KC) for s in range(NS)]
        o = NS * XT
        x_high = [region_b[:, o + s * XT:o + s * XT + KC * PIX].rearrange("p (k n) -> p k n", k=KC) for s in range(NS)]
        x_low = [region_b[:, o + s * XT + KC * PIX:o + (s + 1) * XT].rearrange("p (k n) -> p k n", k=KC)
                 for s in range(NS)]
        o += NS * XT
        v_tile = [region_b[:, o + s * XT:o + (s + 1) * XT].rearrange("p (r k t c) -> p r k t c", r=R, k=KC, t=2)
                  for s in range(NS)]
        o += NS * XT
        stat_tile = [region_b[:, o + s * XT:o + (s + 1) * XT].bitcast(F32).rearrange("p (k n) -> p k n", k=KC)
                     for s in range(NS)]

        at = [H * W // 2]

        def carve(n):
            at[0] += n
            return region_c[:, at[0] - n:at[0]]

        qk_wide = carve(PIX)
        q_low_stage = [carve(PIX // 2).bitcast(F16) for _ in range(NS)]
        bn = carve(KC * NG * 6).rearrange("p (k g s) -> p k g s", k=KC, g=NG)
        p_wide = [carve(UR * P) for _ in range(NS)]
        exp_junk = [p_wide[0][:, q * P:(q + 1) * P] for q in range(NS * R)]
        shifted = [p_wide[1][:, u * PIX:(u + 1) * PIX] for u in range(2)]
        mx = [carve(P), carve(P)]
        zs = [carve(P), carve(P)]
        neg_max = carve(S * R)
        row_neg_max = carve(NS * R)
        m_all = carve(P)
        shift2 = carve(2 * P)
        grown = carve(2 * P)
        z_all = carve(P)
        log_z = carve(P)
        neg_l = [carve(P), carve(P)]
        rest = carve(P)
        neg_l3 = [carve(3 * P // 2).bitcast(BF16).rearrange("p (t n) -> p t n", t=3) for _ in range(2)]
        l_stack = [carve(2 * P).bitcast(BF16).rearrange("p (b n) -> p b n", b=H // BLK) for _ in range(2)]
        assert at[0] <= H * W

        wv_high = region_w[:, 0:KC * C].rearrange("p (k n) -> p k n", k=KC)
        wv_low = region_w[:, KC * C:2 * KC * C].rearrange("p (k n) -> p k n", k=KC)
        o = 2 * KC * C
        wqk_high = region_w[:, o:o + KC * P].rearrange("p (k n) -> p k n", k=KC)
        wqk_low = region_w[:, o + KC * P:o + 2 * KC * P].rearrange("p (k n) -> p k n", k=KC)
        VT = R * 2 * P
        assert S * VT + 2 * PIX <= WLEN
        x_res = ([region_w[:, S * VT:S * VT + 2 * PIX].bitcast(F32)] +
                 [res_tiles[:, j * PIX:(j + 1) * PIX] for j in range(NX - 1)])
        v_ring = [region_w[:, s * VT:(s + 1) * VT].rearrange("p (r t c) -> p r t c", r=R, t=2) for s in range(S)]

        bank4 = ctx.enter_context(nc.psum_tensor("bank4", [P, S, 512], F32))
        bank_qk = ctx.enter_context(nc.psum_tensor("bank_qk", [P, 512], F32))
        bank_row = ctx.enter_context(nc.psum_tensor("bank_row", [P, 512], F32))
        bank_s = ctx.enter_context(nc.psum_tensor("bank_s", [P, 512], F32))

        const_in = sem("const_in")
        w_split = sem("w_split")
        w_stored = sem("w_stored")
        w_in = sem("w_in")
        x_in = [sem(f"x_in{s}") for s in range(NS)]
        stat_in = [sem(f"stat_in{s}") for s in range(NS)]
        stat_free = [sem(f"stat_free{s}") for s in range(NS)]
        stat_dve = sem("stat_dve")
        stat_pe = sem("stat_pe")
        stat_act = sem("stat_act")
        pool_chain = sem("pool_chain")
        parts_ready = [sem(f"parts_ready{s}") for s in range(NS)]
        qk_done = sem("qk_done")
        qk_wide_ready = sem("qk_wide_ready")
        qk_split = sem("qk_split")
        qh_ready = sem("qh_ready")
        qk_moved = [sem(f"qk_moved{s}") for s in range(NS)]
        v_done = sem("v_done")
        vh_ready = sem("vh_ready")
        v_stored = [sem(f"v_stored{s}") for s in range(NS)]
        bank_free = [sem(f"bank_free{s}") for s in range(S)]
        row_score_done = sem("row_score_done")
        row_max_ready = sem("row_max_ready")
        row_negmax_ready = sem("row_negmax_ready")
        row_exp_done = sem("row_exp_done")
        score_done = sem("score_done")
        exps_ready = sem("exps_ready")
        sums_done = sem("sums_done")
        max_ready = sem("max_ready")
        negmax_ready = sem("negmax_ready")
        expsum_done = sem("expsum_done")
        join_dve = sem("join_dve")
        join_pe = sem("join_pe")
        join_act = sem("join_act")
        stack_out = [sem(f"stack_out{d}") for d in range(2)]
        stack_in = sem("stack_in")
        logit_done = sem("logit_done")
        exp_done = [sem(f"exp_done{s}") for s in range(NS)]
        ph_ready = sem("ph_ready")
        p_free = [sem(f"p_free{s}") for s in range(NS)]
        v_in = [sem(f"v_in{s}") for s in range(S)]
        att_done = [sem(f"att_done{s}") for s in range(S)]
        x_res_in = [sem(f"x_res_in{t}") for t in range(NX)]
        x_res_free = [sem(f"x_res_free{t}") for t in range(NX)]
        x_added = sem("x_added")
        bias_set = sem("bias_set")
        table_set = sem("table_set")
        pace = {e: sem(f"pace_{e}") for e in ("sp", "pool", "dve", "pe")}
        acc_out = [sem(f"acc_out{s}") for s in range(S)]

        CONSTS = 9 * 16
        JOIN_DVE, JOIN_PE, JOIN_ACT = 19, 2, 2
        STAT_DVE, STAT_PE = 14, 2
        V_AHEAD = NS * R
        BANK_PROJ, BANK_SCORE, BANK_ATT = NG, NT, KC * 2 * NT
        STORED = 16 * NT
        X_RES = [len(range(t, NG, NX)) for t in range(NX)]
        BANK_ALL = BANK_PROJ + BANK_SCORE + BANK_ATT

        x_pix = x.rearrange("b (k p) h w -> b p k (h w)", p=P)
        x_chunk = x.rearrange("b (k p) h w -> b k p h w", p=P)
        out_chunk = out.rearrange("b (k p) h w -> b k p h w", p=P)

        by_row = (q_pair, k_high, k_low)
        by_column = tuple(t.rearrange("p h w -> p w h") for t in by_row)

        def line(t, fixed, moving, n=1):
            part = t[:, fixed:, :][:, bass.ds(moving, n), :]
            return part.rearrange("p a n -> p (a n)") if n == 1 else part

        def per_image(eng, body):
            if NB > 1:
                with eng.Fori(0, NB - 1) as b:
                    body(b, True)
            body(NB - 1, False)

        def stand(eng, name):
            eng.sem_inc(pace[name], 1)

        block = ctx.enter_context(nc.Block())

        @block.sync
        def _(sp):
            sp.dma_start(b32[:, 0:KC * C].rearrange("p (k n) -> p k n", k=KC),
                         wv_t.rearrange("(k p) n -> p k n", p=P)).then_inc(const_in, 16)
            sp.dma_start(b32[:, KC * C:KC * C + KC * P].rearrange("p (k n) -> p k n", k=KC),
                         wqk_t.rearrange("(k p) n -> p k n", p=P)).then_inc(const_in, 16)
            t = KC * C + KC * P
            sp.dma_start(ident_f[:], ident).then_inc(const_in, 16)
            sp.dma_start(group_f[:], group_mean).then_inc(const_in, 16)
            sp.dma_start(b32[:, t:t + P], far_diag).then_inc(const_in, 16)
            sp.dma_start(b32[:, t + P:t + P + BLK], onehot).then_inc(const_in, 16)
            sp.dma_start(bqk_s, bqk.rearrange("(p a) -> p a", a=1)).then_inc(const_in, 16)
            sp.dma_start(bv_s, bv).then_inc(const_in, 16)
            sp.dma_start(b32[:, t + P + BLK:t + P + BLK + P], ident).then_inc(const_in, 16)
            sp.wait_ge(w_split, 3)
            sp.dma_start(w_dram, region_w[:]).then_inc(w_stored, 16)
            sp.wait_ge(w_stored, 16)

            def stat_load(b, i, s):
                sp.wait_ge(stat_free[s], b * NI + i + 1)
                sp.dma_start(stat_tile[s], x_pix[b][:, :, bass.ds((i * NS + s) * PIX, PIX)]
                             ).then_inc(stat_in[s], 16)

            with sp.Fori(0, NI) as i:
                for s in range(NS):
                    stat_load(0, i, s)

            def image(b, more):
                with sp.Fori(0, NI) as i:
                    for s in range(NS):
                        sp.wait_ge(parts_ready[s], b * NI + i + 1)
                        sp.dma_start(x_tile[s], x_pix[b][:, :, bass.ds((i * NS + s) * PIX, PIX)]
                                     ).then_inc(x_in[s], 16)
                        if more:
                            stat_load(b + 1, i, s)
                for d in range(2):
                    sp.wait_ge(join_dve, b * JOIN_DVE + (13 if d == 0 else 19))
                    sp.dma_start(l_dram[d].rearrange("t h w -> h t w"), neg_l3[d]).then_inc(stack_out[d], 16)
                for d in range(2):
                    sp.wait_ge(stack_out[d], 16 * b + 16)
                    for part in range(3):
                        sp.dma_start(l_stack[d][part * BLK:(part + 1) * BLK],
                                     l_dram[d][part].rearrange("(k h) w -> h k w", h=BLK)).then_inc(stack_in, 16)
                for s in range(NS):
                    sp.wait_ge(v_stored[s], 16 * NI * (b + 1) + 16)
                stand(sp, "sp")
                with sp.Fori(0, KC) as c:
                    m = b * KC + c

                    def load_x(u):
                        t = u % NX
                        sp.wait_ge(x_res_free[t], m * X_RES[t] + u // NX + 1)
                        sp.dma_start(x_res[t].rearrange("p (r w) -> p r w", r=R),
                                     x_chunk[b][c][:, u * R:(u + 1) * R, :]).then_inc(x_res_in[t], 16)

                    for d in (1, 0):
                        src = v_dram.rearrange("h w c -> w h c") if d == 0 else v_dram
                        for u in range(NG):
                            s = u % S
                            sp.wait_ge(att_done[s], (m * 2 + 1 - d) * NT + u // S + 1)
                            sp.dma_start(v_ring[s].rearrange("p r t c -> p r (t c)"),
                                         src[:, u * R:(u + 1) * R, bass.ds(c * 2 * P, 2 * P)]
                                         ).then_inc(v_in[s], 16)
                            if d == 1 and u >= NG - NX:
                                load_x(u - (NG - NX))
                            elif d == 0 and u + NX < NG:
                                load_x(u + NX)

            per_image(sp, image)

        @block.gpsimd
        def _(pool):
            def image(b, more):
                pool.wait_ge(stat_dve, (b + 1) * STAT_DVE)
                stand(pool, "pool")
                with pool.Fori(0, NI) as i:
                    n = b * NI + i
                    for s in range(NS):
                        base = (n * NS + s) * 2 * KC
                        pool.wait_ge(x_in[s], 16 * n + 16)
                        pool.wait_ge(v_done, (n * NS + s) * R + R)
                        stand(pool, "pool")
                        for k in range(KC):
                            nc.gpsimd.tensor_scalar(x_high[s][:, k], x_tile[s][:, k], norm_scale[:, k:k + 1],
                                                    norm_bias[:, k:k + 1], ALU.mult, ALU.add).then_inc(pool_chain, 1)
                        pool.wait_ge(pool_chain, base + KC)
                        stand(pool, "pool")
                        for k in range(KC):
                            nc.gpsimd.tensor_scalar(x_tile[s][:, k], x_tile[s][:, k], norm_scale[:, k:k + 1],
                                                    norm_bias[:, k:k + 1], ALU.mult, ALU.add).then_inc(pool_chain, 1)
                        pool.wait_ge(pool_chain, base + 2 * KC)
                        nc.gpsimd.tensor_tensor(x_low[s], x_tile[s], x_high[s], ALU.subtract
                                                ).then_inc(parts_ready[s], 1)

                with pool.Fori(0, KC) as c:
                    m = b * KC + c
                    for s in range(S):
                        pool.wait_ge(bank_free[s], b * BANK_ALL + BANK_PROJ + BANK_SCORE + (c * 2 + 1) * NT + 1)
                    for u in range(NG):
                        t = u % NX
                        pool.wait_ge(x_res_in[t], 16 * (m * X_RES[t] + u // NX + 1))
                        part = acc[:, u * R:(u + 1) * R, :].rearrange("p r w -> p (r w)")
                        nc.gpsimd.tensor_tensor(part, part, x_res[t], ALU.add).then_inc(x_res_free[t], 1)
                        pool.wait_ge(x_res_free[t], m * X_RES[t] + u // NX + 2)
                        pool.sem_inc(x_added, 1)

            for s in range(NS):
                pool.sem_inc(parts_ready[s], 1)
            for t in range(NX):
                pool.sem_inc(x_res_free[t], 1)
            per_image(pool, image)

        @block.tensor
        def _(pe):
            for s in range(NS):
                pe.sem_inc(exp_done[s], 1)
            pe.sem_inc(v_done, V_AHEAD)
            for s in range(S):
                pe.sem_inc(att_done[s], 1)
                pe.sem_inc(bank_free[s], 1)

            def three(dst, left, right, n_k):
                for k in range(n_k):
                    pe.matmul(dst, left[0](k), right[0](k), start=(k == 0), stop=False)
                    pe.matmul(dst, left[0](k), right[1](k), start=False, stop=False)
                    last = pe.matmul(dst, left[1](k), right[0](k), start=False, stop=(k == n_k - 1))
                return last

            def statistics(b):
                pe.wait_ge(stat_dve, b * STAT_DVE + 2)
                pe.matmul(bank_s[:, 0:KC], group_f[:], small[:, 0, :], start=True, stop=True).then_inc(stat_pe, 1)
                pe.wait_ge(stat_dve, b * STAT_DVE + 6)
                pe.matmul(bank_s[:, KC:2 * KC], group_f[:], small[:, 4, :], start=True, stop=True
                          ).then_inc(stat_pe, 1)

            def image(b, more):
                pe.wait_ge(w_in, 16 * b + 16)
                stand(pe, "pe")
                with pe.Fori(0, NI) as i:
                    n = b * NI + i
                    for s in range(NS):
                        g = n * NS + s
                        pe.wait_ge(parts_ready[s], n + 2)
                        pe.wait_ge(qk_wide_ready, g + 1)
                        three(bank_qk[:], (lambda k: wqk_high[:, k], lambda k: wqk_low[:, k]),
                              (lambda k: x_high[s][:, k], lambda k: x_low[s][:, k]), KC).then_inc(qk_done, 1)
                        for r in range(R):
                            px = slice(r * W, (r + 1) * W)
                            pe.wait_ge(bank_free[r], b * BANK_ALL + i * NS + s + 1)
                            last = three(bank4[:, r], (lambda k: x_high[s][:, k, px], lambda k: x_low[s][:, k, px]),
                                         (lambda k: wv_high[:, k], lambda k: wv_low[:, k]), KC)
                            last.then_inc(v_done, 1)
                        pe.wait_ge(qk_moved[s], MOVE * n + 2 * MOVE)
                        pe.wait_ge(row_exp_done, g + 1)
                        for r in range(R):
                            at = s * R + r
                            q, kh, kl = (line(t, at, i * NS * R) for t in (q_pair, k_high, k_low))
                            dst = bank_row[:, r * P:(r + 1) * P]
                            pe.matmul(dst, q, kh, start=True, stop=False)
                            last = pe.matmul(dst, q, kl, start=False, stop=True)
                        last.then_inc(row_score_done, 1)
                if more:
                    statistics(b + 1)

                with pe.Fori(0, NT) as i:
                    for s in range(S):
                        pe.wait_ge(bank_free[s], b * BANK_ALL + BANK_PROJ + i + 1)
                        for r in range(R):
                            q, kh, kl = (line(t, s * R + r, i * S * R) for t in by_column)
                            dst = bank4[:, s, r * P:(r + 1) * P]
                            pe.matmul(dst, q, kh, start=True, stop=False)
                            pe.matmul(dst, q, kl, start=False, stop=False)
                            last = pe.matmul(dst, ident_b[:], far_b[:], start=False, stop=True)
                        last.then_inc(score_done, 1)

                for s in range(S):
                    pe.wait_ge(bank_free[s], b * BANK_ALL + BANK_PROJ + BANK_SCORE + 1)
                pe.wait_ge(row_exp_done, NG * (b + 1) + 1)
                pe.transpose(bank_s[:, 0:P], mx[0], ident_f[:])
                pe.transpose(bank_s[:, P:2 * P], zs[0], ident_f[:]).then_inc(join_pe, 1)
                pe.wait_ge(join_dve, b * JOIN_DVE + 8)
                pe.transpose(bank_s[:, 2 * P:3 * P], neg_l[0], ident_f[:]).then_inc(join_pe, 1)

                for s in range(S):
                    pe.wait_ge(bank_free[s], b * BANK_ALL + BANK_PROJ + BANK_SCORE + 1)
                pe.wait_ge(stack_in, (b + 1) * 2 * 3 * 16)
                stand(pe, "pe")
                for d in (1, 0):
                    with pe.Fori(0, H // BLK) as blk:
                        shifts = l_stack[d][0:3 * BLK, bass.ds(blk, 1), :].rearrange("p a n -> p (a n)")
                        for u in range(BLK // UR):
                            s = u % NS
                            pe.wait_ge(exp_done[s],
                                       ((b * 2 + (1 - d)) * (H // BLK) + blk) * (BLK // UR // NS) + u // NS + 1)
                            for r in range(UR):
                                q, kh, kl = (line(t, u * UR + r, blk * BLK) for t in (by_row, by_column)[d])
                                dst = bank4[:, s * 2 + r // R, (r % R) * P:(r % R + 1) * P]
                                hot = onehot_b[0:3 * BLK, u * UR + r:u * UR + r + 1].to_broadcast([3 * BLK, P])
                                pe.matmul(dst, kh, q, start=True, stop=False)
                                pe.matmul(dst, kl, q, start=False, stop=False)
                                if d == 1:
                                    pe.matmul(dst, ident_b[:], far_b[:], start=False, stop=False)
                                last = pe.matmul(dst, hot, shifts, start=False, stop=True)
                            last.then_inc(logit_done, 1)

                for s in range(NS):
                    pe.wait_ge(p_free[s], (b + 1) * 2 * (H // UR // NS) + 1)
                stand(pe, "pe")
                with pe.Fori(0, KC) as c:
                    for d in (1, 0):
                        probs = prob_row if d == 0 else prob_col
                        for u in range(NG):
                            s = u % S
                            m = (c * 2 + 1 - d) * NT + u // S
                            pe.wait_ge(v_in[s], 16 * (b * KC * 2 * NT + m) + 16)
                            pe.wait_ge(bank_free[s], b * BANK_ALL + BANK_PROJ + BANK_SCORE + m + 1)
                            for r in range(R):
                                ph, pl = (probs[:, u * R + r, t, :] for t in range(2))
                                last = three(bank4[:, s, r * P:(r + 1) * P],
                                             (lambda k: v_ring[s][:, r, 0], lambda k: v_ring[s][:, r, 1]),
                                             (lambda k: ph, lambda k: pl), 1)
                            last.then_inc(att_done[s], 1)

            statistics(0)
            pe.sem_inc(qk_wide_ready, 1)
            pe.sem_inc(row_exp_done, 1)
            per_image(pe, image)

        @block.scalar
        def _(act):
            for s in range(NS):
                act.sem_inc(v_stored[s], 16)
                act.sem_inc(p_free[s], 1)
            for s in range(S):
                act.sem_inc(acc_out[s], 16)

            def statistics(b):
                act.wait_ge(stat_dve, b * STAT_DVE + 7)
                nc.scalar.activation(small[:, 6, :], small[:, 5, :], ACT.Sqrt).then_inc(stat_act, 1)

            def image(b, more):
                for s in range(S):
                    act.wait_ge(att_done[s], b * KC * 2 * NT + 1)
                act.wait_ge(x_res_free[0], b * KC * X_RES[0] + 1)
                act.dma_start(region_w[:], w_dram).then_inc(w_in, 16)
                for s in range(S):
                    act.wait_ge(acc_out[s], STORED * b * KC + 16)
                nc.scalar.activation(scratch1, bqk_s, ACT.Exp).then_inc(table_set, 1)
                act.wait_ge(table_set, 2 * b + 1)
                with act.Fori(0, NI) as i:
                    n = b * NI + i
                    for s in range(NS):
                        g = n * NS + s
                        act.wait_ge(qk_done, g + 1)
                        nc.scalar.activation(qk_wide, bank_qk[:], ACT.Identity, bias=bqk_s, scale=PROJ_DOWN
                                             ).then_inc(qk_wide_ready, 1)
                        act.wait_ge(v_stored[s], 16 * n + 16)
                        act.wait_ge(qk_split, g + 1)
                        rows = bass.ds((i * NS + s) * R, R)
                        act.dma_start(qk_rows[CQ:P, rows, 0, :],
                                      q_low_stage[s][0:CQ].rearrange("p (r w) -> p r w", r=R)
                                      ).then_inc(qk_moved[s], 16)
                        act.dma_start(qk_rows[0:CQ, rows, 1, :], qk_rows[CQ:P, rows, 1, :]).then_inc(qk_moved[s], 16)
                        act.dma_start(k_low[0:CQ, rows, :], k_low[CQ:P, rows, :]).then_inc(qk_moved[s], 16)
                        for r in range(R):
                            act.wait_ge(v_done, V_AHEAD + g * R + r + 1)
                            nc.scalar.activation(v_tile[s][:, r, :, 0, :],
                                                 bank4[:, r].rearrange("p (k c) -> p k c", k=KC),
                                                 ACT.Copy, scale=PROJ_DOWN).then_inc(vh_ready, 1)
                        for r in range(R):
                            act.wait_ge(bank_free[r], b * BANK_ALL + i * NS + s + 2)
                        act.dma_start(v_dram[bass.ds((i * NS + s) * R, R)].rearrange("r w c -> w r c"),
                                      v_tile[s].rearrange("p r k t c -> p r (k t c)")).then_inc(v_stored[s], 16)
                        act.wait_ge(row_negmax_ready, g + 1)
                        for r in range(R):
                            q = s * R + r
                            ins = nc.scalar.activation(exp_junk[q], bank_row[:, r * P:(r + 1) * P], ACT.Exp,
                                                       bias=row_neg_max[:, q:q + 1],
                                                       accum_out=zs[0][:, q:][:, bass.ds(i * NS * R, 1)])
                        ins.then_inc(row_exp_done, 1)
                if more:
                    statistics(b + 1)

                act.wait_ge(row_exp_done, NG * (b + 1) + 1)
                with act.Fori(0, NT) as i:
                    n = b * NT + i
                    for s in range(0, S, 2):
                        act.wait_ge(negmax_ready, n * 2 + s // 2 + 1)
                        for r in range(R):
                            q = s * R + r
                            ins = nc.scalar.activation(exp_junk[s * R // 2 + r], bank4[:, s, r * P:(r + 1) * P], ACT.Exp,
                                                       bias=neg_max[:, q:q + 1],
                                                       accum_out=zs[1][:, q:][:, bass.ds(i * S * R, 1)])
                        ins.then_inc(bank_free[s], 1)
                        act.wait_ge(bank_free[s + 1], b * BANK_ALL + BANK_PROJ + i + 2)
                        nc.scalar.activation(shifted[s // 2], shifted[s // 2], ACT.Exp).then_inc(exps_ready, 1)

                act.wait_ge(join_dve, b * JOIN_DVE + 3)
                nc.scalar.activation(grown, shift2, ACT.Exp).then_inc(join_act, 1)
                act.wait_ge(join_dve, b * JOIN_DVE + 6)
                nc.scalar.activation(log_z, z_all, ACT.Ln).then_inc(join_act, 1)
                nc.scalar.activation(scratch1, bqk_s, ACT.Exp).then_inc(table_set, 1)
                act.wait_ge(table_set, 2 * b + 2)

                for d in (1, 0):
                    with act.Fori(0, H // UR // NS) as i:
                        n = (b * 2 + (1 - d)) * (H // UR // NS) + i
                        for s in range(NS):
                            act.wait_ge(logit_done, n * NS + s + 1)
                            act.wait_ge(p_free[s], n + 1)
                            nc.scalar.activation(p_wide[s], bank4[:, 2 * s:2 * s + 2, :].rearrange("p a n -> p (a n)"),
                                                 ACT.Exp).then_inc(exp_done[s], 1)

                for s in range(NS):
                    act.wait_ge(p_free[s], (b + 1) * 2 * (H // UR // NS) + 1)
                with act.Fori(0, KC) as c:
                    m = b * KC + c
                    nc.scalar.activation(bv_now, bv_s[:, bass.ds(c, 1)], ACT.Copy).then_inc(bias_set, 1)
                    act.wait_ge(bias_set, m + 1)
                    for s in range(S):
                        act.wait_ge(acc_out[s], STORED * m + 16)
                    for u in range(NG):
                        s = u % S
                        act.wait_ge(att_done[s], m * 2 * NT + u // S + 2)
                        nc.scalar.activation(acc[:, :, u * R:(u + 1) * R],
                                             bank4[:, s].rearrange("p (r n) -> p n r", r=R), ACT.Identity,
                                             bias=bv_now, scale=ATT_DOWN).then_inc(bank_free[s], 1)
                    for u in range(NG):
                        s = u % S
                        act.wait_ge(bank_free[s], b * BANK_ALL + BANK_PROJ + BANK_SCORE + (c * 2 + 1) * NT + u // S + 2)
                        act.dma_start(out_chunk[b][c][:, u * R:(u + 1) * R, :], acc[:, u * R:(u + 1) * R, :]
                                      ).then_inc(acc_out[s], 16)

            statistics(0)
            per_image(act, image)
            for s in range(S):
                act.wait_ge(acc_out[s], STORED * NB * KC + 16)

        @block.vector
        def _(dve):
            for s in range(NS):
                dve.sem_inc(stat_free[s], 1)
                dve.sem_inc(qk_moved[s], MOVE)

            dve.wait_ge(const_in, CONSTS)
            wide = b32[:, 0:KC * C + KC * P]
            nc.vector.tensor_scalar(wide, wide, W_SCALE, None, ALU.mult).then_inc(w_split, 1)
            dve.wait_ge(w_split, 1)
            wv_wide, wqk_wide = b32[:, 0:KC * C], b32[:, KC * C:KC * C + KC * P]
            wvh, wvl = region_w[:, 0:KC * C], region_w[:, KC * C:2 * KC * C]
            o = 2 * KC * C
            wqh, wql = region_w[:, o:o + KC * P], region_w[:, o + KC * P:o + 2 * KC * P]
            t = KC * C + KC * P
            nc.vector.tensor_copy(far_b[:], b32[:, t:t + P])
            nc.vector.tensor_copy(onehot_b[:], b32[:, t + P:t + P + BLK])
            nc.vector.tensor_copy(ident_b[:], b32[:, t + P + BLK:t + P + BLK + P])
            nc.vector.tensor_copy(wvh, wv_wide)
            nc.vector.tensor_copy(wqh, wqk_wide).then_inc(w_split, 1)
            dve.wait_ge(w_split, 2)
            nc.vector.tensor_tensor(wvl, wv_wide, wvh, ALU.subtract)
            nc.vector.tensor_tensor(wql, wqk_wide, wqh, ALU.subtract).then_inc(w_split, 1)

            def stat_group(b, i, s):
                dve.wait_ge(stat_in[s], 16 * (b * NI + i) + 16)
                for k in range(KC):
                    last = nc.vector.bn_stats(bn[:, k, bass.ds(i * NS + s, 1), :].rearrange("p a s -> p (a s)"),
                                              stat_tile[s][:, k])
                last.then_inc(stat_free[s], 1)

            def statistics(b):
                count = [0]

                def link(ins):
                    ins.then_inc(stat_dve, 1)
                    count[0] += 1
                    dve.wait_ge(stat_dve, b * STAT_DVE + count[0])

                for s in range(NS):
                    dve.wait_ge(stat_free[s], (b + 1) * NI + 1)
                stand(dve, "dve")
                for k in range(KC):
                    last = nc.vector.bn_aggr(small[:, 8 + 0:10, :].rearrange("p a k -> p (a k)")[:, 2 * k:2 * k + 2],
                                             bn[:, k].rearrange("p g s -> p (g s)"))
                link(last)
                mv = small[:, 8:10, :].rearrange("p a k -> p (a k)").rearrange("p (k t) -> p t k", t=2)
                mean, mean_g, d, d2, mom, var_g, sd, y = (small[:, j, :] for j in range(8))
                link(nc.vector.tensor_copy(mean, mv[:, 0, :]))
                dve.wait_ge(stat_pe, STAT_PE * b + 1)
                link(nc.vector.tensor_copy(mean_g, bank_s[:, 0:KC]))
                link(nc.vector.tensor_tensor(d, mean, mean_g, ALU.subtract))
                link(nc.vector.tensor_tensor(d2, d, d, ALU.mult))
                link(nc.vector.tensor_tensor(mom, d2, mv[:, 1, :], ALU.add))
                dve.wait_ge(stat_pe, STAT_PE * b + 2)
                link(nc.vector.tensor_scalar(var_g, bank_s[:, KC:2 * KC], EPS, None, ALU.add))
                dve.wait_ge(stat_act, b + 1)
                link(nc.vector.reciprocal(y, sd))
                link(nc.vector.tensor_tensor(d, y, y, ALU.mult))
                link(nc.vector.tensor_tensor(d2, d, var_g, ALU.mult))
                link(nc.vector.tensor_scalar(d, d2, -0.5, 1.5, ALU.mult, ALU.add))
                link(nc.vector.tensor_tensor(d2, y, d, ALU.mult))
                link(nc.vector.tensor_scalar(norm_scale, d2, X_SCALE, None, ALU.mult))
                link(nc.vector.scalar_tensor_tensor(out=norm_bias, in0=mean_g, scalar=-1.0,
                                                    in1=norm_scale, op0=ALU.mult, op1=ALU.mult))
                stand(dve, "dve")
                assert count[0] == STAT_DVE

            def image(b, more):
                for s in range(S):
                    dve.wait_ge(acc_out[s], STORED * b * KC + 16)
                stand(dve, "dve")
                with dve.Fori(0, NI) as i:
                    n = b * NI + i
                    for s in range(NS):
                        g = n * NS + s
                        rows = bass.ds((i * NS + s) * R, R)
                        wide_q = qk_wide[0:CQ].rearrange("p (r w) -> p r w", r=R)
                        wide_k = qk_wide[CQ:P].rearrange("p (r w) -> p r w", r=R)
                        dve.wait_ge(qk_moved[s], MOVE * n + MOVE)
                        dve.wait_ge(qk_wide_ready, g + 2)
                        nc.vector.tensor_copy(qk_rows[0:CQ, rows, 0, :], wide_q).then_inc(qh_ready, 1)
                        nc.vector.tensor_copy(qk_rows[CQ:P, rows, 1, :], wide_k).then_inc(qh_ready, 1)
                        dve.wait_ge(qh_ready, 2 * g + 2)
                        nc.vector.tensor_tensor(q_low_stage[s][0:CQ].rearrange("p (r w) -> p r w", r=R), wide_q,
                                                qk_rows[0:CQ, rows, 0, :], ALU.subtract)
                        nc.vector.tensor_tensor(k_low[CQ:P, rows, :], wide_k, qk_rows[CQ:P, rows, 1, :],
                                                ALU.subtract).then_inc(qk_split, 1)
                        for r in range(R):
                            dve.wait_ge(vh_ready, g * R + r + 1)
                            bank = bank4[:, r].rearrange("p (k c) -> p k c", k=KC)
                            nc.vector.scalar_tensor_tensor(out=v_tile[s][:, r, :, 1, :], in0=bank, scalar=PROJ_DOWN,
                                                           in1=v_tile[s][:, r, :, 0, :], op0=ALU.mult,
                                                           op1=ALU.subtract).then_inc(bank_free[r], 1)
                        dve.wait_ge(row_score_done, g + 1)
                        nc.vector.tensor_reduce(mx[0][:, s * R:][:, bass.ds(i * NS * R, R)],
                                                bank_row[:].rearrange("p (r n) -> p r n", r=R),
                                                AXX, ALU.max).then_inc(row_max_ready, 1)
                        dve.wait_ge(row_max_ready, g + 1)
                        dve.wait_ge(row_exp_done, g + 1)
                        nc.vector.tensor_scalar(row_neg_max[:, s * R:(s + 1) * R],
                                                mx[0][:, s * R:][:, bass.ds(i * NS * R, R)], -1.0, None,
                                                ALU.mult).then_inc(row_negmax_ready, 1)
                        if more:
                            stat_group(b + 1, i, s)
                if more:
                    statistics(b + 1)

                with dve.Fori(0, NT) as i:
                    n = b * NT + i
                    for s in range(S):
                        u = n * S + s
                        scores = bank4[:, s].rearrange("p (r n) -> p r n", r=R)
                        tops = mx[1][:, s * R:][:, bass.ds(i * S * R, R)]
                        dve.wait_ge(score_done, u + 1)
                        nc.vector.tensor_reduce(tops, scores, AXX, ALU.max).then_inc(max_ready, 1)
                        dve.wait_ge(max_ready, u + 1)
                        if s % 2 == 0:
                            dve.wait_ge(bank_free[s], b * BANK_ALL + BANK_PROJ + i + 1)
                            nc.vector.tensor_scalar(neg_max[:, s * R:(s + 1) * R], tops, -1.0, None,
                                                    ALU.mult).then_inc(negmax_ready, 1)
                        else:
                            nc.vector.tensor_tensor(shifted[s // 2].rearrange("p (r n) -> p r n", r=R), scores,
                                                    tops.unsqueeze(2).broadcast_to([P, R, P]),
                                                    ALU.subtract).then_inc(bank_free[s], 1)
                        if s >= 2:
                            w = s - 2
                            dve.wait_ge(exps_ready, n * 2 + w + 1)
                            nc.vector.tensor_reduce(zs[1][:, (2 * w + 1) * R:][:, bass.ds(i * S * R, R)],
                                                    shifted[w].rearrange("p (r n) -> p r n", r=R),
                                                    AXX, ALU.add).then_inc(sums_done, 1)
                    dve.wait_ge(sums_done, n * 2 + 2)

                stand(dve, "dve")

                count = [0]

                def link(ins):
                    ins.then_inc(join_dve, 1)
                    count[0] += 1
                    dve.wait_ge(join_dve, b * JOIN_DVE + count[0])

                def split3(d):
                    link(nc.vector.tensor_copy(neg_l3[d][:, 0, :], neg_l[d]))
                    link(nc.vector.tensor_tensor(rest, neg_l[d], neg_l3[d][:, 0, :], ALU.subtract))
                    link(nc.vector.tensor_copy(neg_l3[d][:, 1, :], rest))
                    link(nc.vector.tensor_tensor(rest, rest, neg_l3[d][:, 1, :], ALU.subtract))
                    link(nc.vector.tensor_copy(neg_l3[d][:, 2, :], rest))

                dve.wait_ge(join_pe, b * JOIN_PE + 1)
                link(nc.vector.tensor_tensor(m_all, bank_s[:, 0:P], mx[1], ALU.max))
                link(nc.vector.tensor_tensor(shift2[:, 0:P], bank_s[:, 0:P], m_all, ALU.subtract))
                link(nc.vector.tensor_tensor(shift2[:, P:2 * P], mx[1], m_all, ALU.subtract))
                dve.wait_ge(join_act, b * JOIN_ACT + 1)
                link(nc.vector.tensor_tensor(z_all, bank_s[:, P:2 * P], grown[:, 0:P], ALU.mult))
                link(nc.vector.tensor_tensor(rest, zs[1], grown[:, P:2 * P], ALU.mult))
                link(nc.vector.tensor_tensor(z_all, z_all, rest, ALU.add))
                dve.wait_ge(join_act, b * JOIN_ACT + 2)
                link(nc.vector.tensor_tensor(rest, m_all, log_z, ALU.add))
                link(nc.vector.tensor_scalar(neg_l[0], rest, -1.0, P_SCALE_LOG2 * log(2.0),
                                             ALU.mult, ALU.add))
                split3(0)
                dve.wait_ge(join_pe, b * JOIN_PE + 2)
                link(nc.vector.tensor_copy(neg_l[1], bank_s[:, 2 * P:3 * P]))
                split3(1)
                assert count[0] == JOIN_DVE

                for s in range(NS):
                    dve.wait_ge(v_stored[s], 16 * NI * (b + 1) + 16)
                stand(dve, "dve")
                for d in (1, 0):
                    probs = prob_col if d == 1 else prob_row
                    with dve.Fori(0, H // UR // NS) as i:
                        n = (b * 2 + (1 - d)) * (H // UR // NS) + i
                        for s in range(NS):
                            u = n * NS + s
                            high, low = (line(probs[:, :, t, :], s * UR, i * NS * UR, UR) for t in range(2))
                            src = p_wide[s].rearrange("p (r n) -> p r n", r=UR)
                            dve.wait_ge(exp_done[s], n + 2)
                            nc.vector.tensor_copy(high, src).then_inc(ph_ready, 1)
                            dve.wait_ge(ph_ready, u + 1)
                            nc.vector.tensor_tensor(low, src, high, ALU.subtract).then_inc(p_free[s], 1)

                with dve.Fori(0, KC) as c:
                    m = b * KC + c
                    for u in range(NG):
                        s = u % S
                        dve.wait_ge(x_added, m * NG + u + 1)
                        dve.wait_ge(att_done[s], (m * 2 + 1) * NT + u // S + 2)
                        part = acc[:, u * R:(u + 1) * R, :]
                        nc.vector.scalar_tensor_tensor(out=part, in0=bank4[:, s].rearrange("p (r n) -> p r n", r=R),
                                                       scalar=ATT_DOWN, in1=part,
                                                       op0=ALU.mult, op1=ALU.add).then_inc(bank_free[s], 1)

            with dve.Fori(0, NI) as i:
                for s in range(NS):
                    stat_group(0, i, s)
            statistics(0)
            per_image(dve, image)


_OUT = "out_dram"


def kernel(x, L0_conv_Wq, L0_conv_bq, L0_conv_Wk, L0_conv_bk, L0_conv_Wv, L0_conv_bv):
    import numpy as np
    import concourse.bacc as bacc
    from concourse.bass_utils import run_bass_kernel_spmd

    G = 16
    B, C, H, W = x.shape
    rows = np.arange(128)
    arrays = {
        "x_dram": np.ascontiguousarray(x),
        "wv_t_dram": np.ascontiguousarray(np.asarray(L0_conv_Wv).T),
        "wqk_t_dram": np.ascontiguousarray(np.concatenate([L0_conv_Wq, L0_conv_Wk], 0).T),
        "bqk_dram": np.concatenate([L0_conv_bq, L0_conv_bk]),
        "bv_dram": np.ascontiguousarray(np.asarray(L0_conv_bv).reshape(C // 128, 128).T),
        "ident_dram": np.eye(128, dtype=np.float32),
        "group_mean_dram": (rows[:, None] // G == rows[None] // G).astype(np.float32) / np.float32(G),
        "onehot_dram": (rows[:, None] % 32 == np.arange(32)[None]).astype(np.float32),
        "far_diag_dram": np.where(np.eye(128, dtype=bool), np.float32(FAR), np.float32(0)).astype(np.float32),
    }
    nc = bacc.Bacc("TRN2", target_bir_lowering=False, num_devices=1)
    args = [nc.dram_tensor(n, a.shape, mybir.dt.from_np(a.dtype), kind="ExternalInput").ap()
            for n, a in arrays.items()]
    args.append(nc.dram_tensor(_OUT, (B, C, H, W), F32, kind="ExternalOutput").ap())
    criss_cross_program(nc, *args)
    r = run_bass_kernel_spmd(nc, [arrays], core_ids=[0])
    return r.results[0][_OUT]
```

```python
from contextlib import ExitStack
from math import log

import concourse.bass as bass
from concourse import mybir

F32 = mybir.dt.float32
F16 = mybir.dt.float16
BF16 = mybir.dt.bfloat16
ALU = mybir.AluOpType
ACT = mybir.ActivationFunctionType
AXX = mybir.AxisListType.X

P = 128
EPS = 1e-5
X_SCALE = 2.0 ** 5
W_SCALE = 2.0 ** 8
P_SCALE_LOG2 = 12
PROJ_DOWN = 1.0 / (X_SCALE * W_SCALE)
ATT_DOWN = 2.0 ** -P_SCALE_LOG2
FAR = -3.0e38


def criss_cross_program(nc, x, wv_t, wqk_t, bqk, bv, ident, group_mean, onehot, far_diag, out):
    NB, C, H, W = x.shape
    KC = C // P
    CQ = wqk_t.shape[1] // 2
    assert H == P and W == P and 2 * CQ == P
    R = 4
    NG = H // R
    NI = NG // 2
    S = 4
    NT = H // (R * S)
    NS = 2
    PIX = R * W
    FEED = 7
    UR = 8
    UNITS = H // UR
    BLK = 32
    MOVE = 3 * 16

    ctx = ExitStack()
    with ctx:
        def sb(name, shape, dt):
            return ctx.enter_context(nc.sbuf_tensor(name, shape, dt))

        def sem(name):
            return ctx.enter_context(nc.semaphore(name))

        v_dram = nc.dram_tensor("v_scratch", [H, KC, W, 2 * P], F16).ap()
        WLEN = 2 * KC * C + 2 * KC * P
        w_dram = nc.dram_tensor("w_scratch", [P, WLEN], F16).ap()
        l_dram = nc.dram_tensor("shift_scratch", [2, 3, H, W], BF16).ap()

        region_a = sb("region_a", [P, H * 2 * W], F16)
        region_b = sb("region_b", [P, H * 2 * W], F16)
        region_c = sb("region_c", [P, H * W], F32)
        region_w = sb("region_w", [P, WLEN], F16)
        ident_f = sb("ident_f", [P, P], F32)
        group_f = sb("group_f", [P, P], F32)
        ident_b = sb("ident_b", [P, P], BF16)
        far_b = sb("far_b", [P, P], BF16)
        onehot_b = sb("onehot_b", [P, BLK], BF16)
        vectors = sb("vectors", [P, 3 + 3 * KC], F32)
        bqk_s, scratch1, bv_now = (vectors[:, j:j + 1] for j in range(3))
        bv_s, norm_scale, norm_bias = (vectors[:, 3 + j * KC:3 + (j + 1) * KC] for j in range(3))
        feed_tiles = sb("feed_tiles", [P, 2 * PIX], F32)
        small = sb("small", [P, 12, KC], F32)

        qk_rows = region_a[:].rearrange("p (h t w) -> p h t w", h=H, t=2)
        q_pair, k_high = qk_rows[:, :, 0, :], qk_rows[:, :, 1, :]
        prob_row = qk_rows
        prob_col = region_b[:].rearrange("p (w t h) -> p w t h", w=W, t=2)
        acc = region_c[:].rearrange("p (h w) -> p h w", h=H)
        c16 = region_c[:].bitcast(F16)
        k_low = c16[:, 0:H * W].rearrange("p (h w) -> p h w", h=H)

        XT = 2 * KC * PIX
        b32 = region_b[:].bitcast(F32)
        x_tile = [b32[:, s * KC * PIX:(s + 1) * KC * PIX].rearrange("p (k n) -> p k n", k=KC) for s in range(NS)]
        o = NS * XT
        x_high = [region_b[:, o + s * XT:o + s * XT + KC * PIX].rearrange("p (k n) -> p k n", k=KC) for s in range(NS)]
        x_low = [region_b[:, o + s * XT + KC * PIX:o + (s + 1) * XT].rearrange("p (k n) -> p k n", k=KC)
                 for s in range(NS)]
        o += NS * XT
        v_tile = [region_b[:, o + s * XT:o + (s + 1) * XT].rearrange("p (r k t c) -> p r k t c", r=R, k=KC, t=2)
                  for s in range(NS)]
        o += NS * XT
        stat_tile = [region_b[:, o + s * XT:o + (s + 1) * XT].bitcast(F32).rearrange("p (k n) -> p k n", k=KC)
                     for s in range(NS)]

        FIRST = 4
        FT = 2 * KC * PIX
        a32 = region_a[:].bitcast(F32)
        first_tile = [a32[:, j * FT:(j + 1) * FT].rearrange("p (k n) -> p k n", k=KC) for j in range(FIRST)]

        at = [H * W // 2]

        def carve(n):
            at[0] += n
            return region_c[:, at[0] - n:at[0]]

        qk_wide = carve(PIX)
        q_low_stage = [carve(PIX // 2).bitcast(F16) for _ in range(NS)]
        bn = carve(KC * NG * 6).rearrange("p (k g s) -> p k g s", k=KC, g=NG)
        p_wide = [carve(UR * P) for _ in range(NS)]
        exp_junk = [p_wide[0][:, q * P:(q + 1) * P] for q in range(NS * R)]
        shifted = [p_wide[1][:, u * PIX:(u + 1) * PIX] for u in range(2)]
        mx = [carve(P), carve(P)]
        zs = [carve(P), carve(P)]
        neg_max = carve(S * R)
        row_neg_max = carve(NS * R)
        m_all = carve(P)
        shift2 = carve(2 * P)
        grown = carve(2 * P)
        z_all = carve(P)
        log_z = carve(P)
        neg_l = [carve(P), carve(P)]
        rest = carve(P)
        neg_l3 = [carve(3 * P // 2).bitcast(BF16).rearrange("p (t n) -> p t n", t=3) for _ in range(2)]
        l_stack = [carve(2 * P).bitcast(BF16).rearrange("p (b n) -> p b n", b=H // BLK) for _ in range(2)]
        assert at[0] <= H * W

        wv_high = region_w[:, 0:KC * C].rearrange("p (k n) -> p k n", k=KC)
        wv_low = region_w[:, KC * C:2 * KC * C].rearrange("p (k n) -> p k n", k=KC)
        o = 2 * KC * C
        wqk_high = region_w[:, o:o + KC * P].rearrange("p (k n) -> p k n", k=KC)
        wqk_low = region_w[:, o + KC * P:o + 2 * KC * P].rearrange("p (k n) -> p k n", k=KC)
        VT = R * 2 * P
        IN_W = 5
        assert IN_W * VT <= WLEN and IN_W + 2 == FEED and VT == 2 * PIX
        feed = ([region_w[:, t * VT:(t + 1) * VT] for t in range(IN_W)] +
                [feed_tiles[:, t * PIX:(t + 1) * PIX].bitcast(F16) for t in range(FEED - IN_W)])
        v_feed = [t.rearrange("p (r t c) -> p r t c", r=R, t=2) for t in feed]
        x_feed = [t.bitcast(F32) for t in feed]

        banks = ctx.enter_context(nc.psum_tensor("banks", [P, S + 2, 512], F32))
        bank4 = banks[:, 0:S, :]
        bank_qk = banks[:, S, :]
        bank_row = banks[:, S + 1, :]
        PAIRS = (S + 2) // 2
        bank_s = ctx.enter_context(nc.psum_tensor("bank_s", [P, 512], F32))

        const_in = sem("const_in")
        w_stored = sem("w_stored")
        w_in = sem("w_in")
        x_in = [sem(f"x_in{s}") for s in range(NS)]
        stat_in = [sem(f"stat_in{s}") for s in range(NS)]
        first_in = [sem(f"first_in{j}") for j in range(FIRST)]
        qk_moved = [sem(f"qk_moved{s}") for s in range(NS)]
        v_stored = [sem(f"v_stored{s}") for s in range(NS)]
        stack_out = [sem(f"stack_out{d}") for d in range(2)]
        stack_in = [sem(f"stack_in{d}") for d in range(2)]
        feed_in = [sem(f"feed_in{t}") for t in range(FEED)]
        acc_out = [sem(f"acc_out{s}") for s in range(S)]
        stat_free = [sem(f"stat_free{s}") for s in range(NS)]
        first_free = [sem(f"first_free{j}") for j in range(FIRST)]
        stat_dve = sem("stat_dve")
        stat_pe = sem("stat_pe")
        stat_act = sem("stat_act")
        w_split = sem("w_split")
        pool_chain = sem("pool_chain")
        first_parts = sem("first_parts")
        parts_ready = [sem(f"parts_ready{s}") for s in range(NS)]
        qk_done = sem("qk_done")
        qk_wide_ready = sem("qk_wide_ready")
        qh_ready = sem("qh_ready")
        qk_split = sem("qk_split")
        v_done = sem("v_done")
        vh_ready = sem("vh_ready")
        bank_free = [sem(f"bank_free{s}") for s in range(S)]
        row_score_done = sem("row_score_done")
        row_max_ready = sem("row_max_ready")
        row_negmax_ready = sem("row_negmax_ready")
        row_exp_done = sem("row_exp_done")
        score_done = sem("score_done")
        max_ready = sem("max_ready")
        negmax_ready = sem("negmax_ready")
        exps_ready = sem("exps_ready")
        sums_done = sem("sums_done")
        join_dve = sem("join_dve")
        join_pe = sem("join_pe")
        join_act = sem("join_act")
        table_set = sem("table_set")
        logit_done = sem("logit_done")
        exp_done = [sem(f"exp_done{s}") for s in range(NS)]
        ph_ready = sem("ph_ready")
        p_free = [sem(f"p_free{s}") for s in range(NS)]
        att_done = [sem(f"att_done{s}") for s in range(S)]
        bias_set = sem("bias_set")
        x_added = sem("x_added")
        pace = {e: sem(f"pace_{e}") for e in ("sp", "pool", "dve", "pe")}

        CONSTS = 9 * 16
        JOIN_DVE, JOIN_PE, JOIN_ACT = 19, 2, 2
        STAT_DVE, STAT_PE, STAT_ACT = 13, 2, 2
        V_AHEAD = NS * R
        SHIFTED = [u for u in range(NG) if u % 8 in (1, 3, 6)]
        BIASED = [u for u in range(NG) if u not in SHIFTED]
        MEANS_AT, MOMENTS_AT, SQUARES_AT, VARIANCES_AT = (NG // 8 * j for j in (1, 2, 4, 5))
        BANK_PROJ, BANK_SCORE, BANK_ATT = NG, NT, KC * 2 * NT
        STORED = 16 * NT
        FEEDS = [("v", 1, u) for u in range(NG)]
        for u in range(NG):
            FEEDS += [("x", 0, u), ("v", 0, u)]
        FEED_USES = [len(range(t, len(FEEDS), FEED)) for t in range(FEED)]
        BANK_ALL = BANK_PROJ + BANK_SCORE + BANK_ATT

        x_pix = x.rearrange("b (k p) h w -> b p k (h w)", p=P)
        x_chunk = x.rearrange("b (k p) h w -> b k p h w", p=P)
        out_chunk = out.rearrange("b (k p) h w -> b k p h w", p=P)

        by_row = (q_pair, k_high, k_low)
        by_column = tuple(t.rearrange("p h w -> p w h") for t in by_row)

        def line(t, fixed, moving, n=1):
            part = t[:, fixed:, :][:, lanes_at(moving, n), :]
            return part.rearrange("p a n -> p (a n)") if n == 1 else part

        def lanes_at(moving, n):
            return slice(moving, moving + n) if isinstance(moving, int) else bass.ds(moving, n)

        def lanes(t, fixed, moving, n):
            return t[:, fixed:][:, lanes_at(moving, n)]

        def per_image(eng, body):
            if NB > 1:
                with eng.Fori(0, NB - 1) as b:
                    body(b, True)
            body(NB - 1, False)

        def stand(eng, name):
            eng.sem_inc(pace[name], 1)

        def wait_feed(eng, m, kind, d, u):
            at = FEEDS.index((kind, d, u))
            t = at % FEED
            eng.wait_ge(feed_in[t], 16 * (m * FEED_USES[t] + at // FEED + 1))
            return t

        def unit_pair(d, u):
            t = ((1 - d) * UNITS + u) % PAIRS
            return banks[:, 2 * t:2 * t + 2, :]

        def step_done(m, d, u):
            return (m * 2 + 1 - d) * NT + u // S + 2

        block = ctx.enter_context(nc.Block())

        @block.sync
        def _(sp):
            sp.dma_start(b32[:, 0:KC * C].rearrange("p (k n) -> p k n", k=KC),
                         wv_t.rearrange("(k p) n -> p k n", p=P)).then_inc(const_in, 16)
            sp.dma_start(b32[:, KC * C:KC * C + KC * P].rearrange("p (k n) -> p k n", k=KC),
                         wqk_t.rearrange("(k p) n -> p k n", p=P)).then_inc(const_in, 16)

            def stat_load(b, i, s):
                sp.wait_ge(stat_free[s], b * NI + i + 1)
                sp.dma_start(stat_tile[s], x_pix[b + 1][:, :, bass.ds((i * NS + s) * PIX, PIX)]
                             ).then_inc(stat_in[s], 16)

            def first_load(i, j):
                sp.wait_ge(first_free[j], i + 1)
                sp.dma_start(first_tile[j], x_pix[0][:, :, lanes_at((i * FIRST + j) * 2 * PIX, 2 * PIX)]
                             ).then_inc(first_in[j], 16)

            sp.wait_ge(const_in, CONSTS)
            for j in range(FIRST):
                first_load(0, j)
            with sp.Fori(1, NI // FIRST) as i:
                for j in range(FIRST):
                    first_load(i, j)
            sp.wait_ge(w_split, 3)
            sp.dma_start(w_dram, region_w[:]).then_inc(w_stored, 16)
            sp.wait_ge(w_stored, 16)

            def image(b, more):
                def x_load(i, s):
                    sp.wait_ge(parts_ready[s], b * NI + i + 1)
                    sp.dma_start(x_tile[s], x_pix[b][:, :, bass.ds((i * NS + s) * PIX, PIX)]).then_inc(x_in[s], 16)

                x_load(0, 0)
                for s in range(S):
                    sp.wait_ge(att_done[s], b * KC * 2 * NT + 1)
                sp.wait_ge(x_added, (b * KC + 1) * NG)
                sp.dma_start(region_w[:], w_dram).then_inc(w_in, 16)
                x_load(0, 1)
                for s in range(NS):
                    if more:
                        stat_load(b, 0, s)
                with sp.Fori(1, NI) as i:
                    for s in range(NS):
                        x_load(i, s)
                        if more:
                            stat_load(b, i, s)
                for d in (1, 0):
                    sp.wait_ge(join_dve, b * JOIN_DVE + (13 if d == 1 else 19))
                    sp.dma_start(l_dram[d].rearrange("t h w -> h t w"), neg_l3[d]).then_inc(stack_out[d], 16)
                for d in (1, 0):
                    sp.wait_ge(stack_out[d], 16 * b + 16)
                    for part in range(3):
                        sp.dma_start(l_stack[d][part * BLK:(part + 1) * BLK],
                                     l_dram[d][part].rearrange("(k h) w -> h k w", h=BLK)).then_inc(stack_in[d], 16)
                for s in range(NS):
                    sp.wait_ge(v_stored[s], 16 * NI * (b + 1) + 16)
                stand(sp, "sp")
                with sp.Fori(0, KC) as c:
                    m = b * KC + c

                    for at, (kind, d, u) in enumerate(FEEDS):
                        t = at % FEED
                        ago = 0 if at >= FEED else 1
                        kind0, d0, u0 = FEEDS[at - FEED] if not ago else FEEDS[t + (FEED_USES[t] - 1) * FEED]
                        if kind0 == "v":
                            sp.wait_ge(att_done[u0 % S], step_done(m - ago, d0, u0))
                        else:
                            sp.wait_ge(x_added, (m - ago + 1) * NG + u0 + 1)
                        rows = slice(u * R, (u + 1) * R)
                        if kind == "v":
                            chunk = v_dram[:, bass.ds(c, 1)].rearrange("h a w n -> h (a w) n")
                            src = chunk.rearrange("h w n -> w h n") if d == 0 else chunk
                            sp.dma_start(v_feed[t].rearrange("p r t c -> p r (t c)"), src[:, rows]
                                         ).then_inc(feed_in[t], 16)
                        else:
                            sp.dma_start(x_feed[t].rearrange("p (r w) -> p r w", r=R),
                                         x_chunk[b][c][:, rows, :]).then_inc(feed_in[t], 16)

            per_image(sp, image)

        @block.gpsimd
        def _(pool):
            def image(b, more):
                pool.wait_ge(stat_dve, (b + 1) * STAT_DVE)
                stand(pool, "pool")

                def group(i, s):
                    n = b * NI + i
                    base = (b * (NG - 1) + i * NS + s - 1) * 2 * KC
                    pool.wait_ge(x_in[s], 16 * n + 16)
                    pool.wait_ge(v_done, (n * NS + s) * R + R)
                    stand(pool, "pool")
                    for k in range(KC):
                        nc.gpsimd.tensor_scalar(x_high[s][:, k], x_tile[s][:, k], norm_scale[:, k:k + 1],
                                                norm_bias[:, k:k + 1], ALU.mult, ALU.add).then_inc(pool_chain, 1)
                    pool.wait_ge(pool_chain, base + KC)
                    stand(pool, "pool")
                    for k in range(KC):
                        nc.gpsimd.tensor_scalar(x_tile[s][:, k], x_tile[s][:, k], norm_scale[:, k:k + 1],
                                                norm_bias[:, k:k + 1], ALU.mult, ALU.add).then_inc(pool_chain, 1)
                    pool.wait_ge(pool_chain, base + 2 * KC)
                    nc.gpsimd.tensor_tensor(x_low[s], x_tile[s], x_high[s], ALU.subtract
                                            ).then_inc(parts_ready[s], 1)

                for s in range(1, NS):
                    group(0, s)
                with pool.Fori(1, NI) as i:
                    for s in range(NS):
                        group(i, s)

                with pool.Fori(0, KC) as c:
                    m = b * KC + c
                    for s in range(S):
                        pool.wait_ge(bank_free[s], b * BANK_ALL + BANK_PROJ + BANK_SCORE + (c * 2 + 1) * NT + 1)
                    for u in range(NG):
                        t = wait_feed(pool, m, "x", 0, u)
                        part = acc[:, u * R:(u + 1) * R, :].rearrange("p r w -> p (r w)")
                        nc.gpsimd.tensor_tensor(part, part, x_feed[t], ALU.add).then_inc(x_added, 1)

            for s in range(NS):
                pool.sem_inc(parts_ready[s], 1)
            pool.sem_inc(x_added, NG)
            per_image(pool, image)

        @block.tensor
        def _(pe):
            for s in range(NS):
                pe.sem_inc(exp_done[s], 1)
            pe.sem_inc(v_done, V_AHEAD)
            for s in range(S):
                pe.sem_inc(att_done[s], 1)
                pe.sem_inc(bank_free[s], 1)

            def three(dst, left, right, n_k, between=None):
                passes = [(k, a, c) for k in range(n_k) for a, c in ((0, 0), (0, 1), (1, 0))]
                for at, (k, a, c) in enumerate(passes):
                    last = pe.matmul(dst, left[a](k), right[c](k), start=(at == 0), stop=(at == len(passes) - 1))
                    if between and at < 2 * R:
                        between(at)
                return last

            def stat_sum(b, column, moment, step):
                pe.wait_ge(stat_dve, b * STAT_DVE + step)
                pe.matmul(bank_s[:, 3 * P + column:3 * P + column + KC], group_f[:], small[:, moment, :], start=True,
                          stop=True).then_inc(stat_pe, 1)

            def group_means(b):
                stat_sum(b, 0, 0, 2)

            def group_variances(b):
                stat_sum(b, KC, 4, 6)

            def image(b, more):
                pe.wait_ge(w_in, 16 * b + 16)
                stand(pe, "pe")

                def row_score(i, s, j):
                    r, low = divmod(j, 2)
                    q, k = (line(t, s * R + r, i * NS * R) for t in (q_pair, (k_high, k_low)[low]))
                    last = pe.matmul(bank_row[:, r * P:(r + 1) * P], q, k, start=(low == 0), stop=(low == 1))
                    if j == 2 * R - 1:
                        last.then_inc(row_score_done, 1)

                def wait_row(i, s):
                    n = b * NI + i
                    pe.wait_ge(qk_moved[s], MOVE * n + 2 * MOVE)
                    pe.wait_ge(row_exp_done, n * NS + s + 1)

                def groups(i, first):
                    n = b * NI + i
                    for s in range(NS):
                        g = n * NS + s
                        pe.wait_ge(parts_ready[s], n + 2)
                        pe.wait_ge(qk_wide_ready, g + 1)
                        three(bank_qk, (lambda k: wqk_high[:, k], lambda k: wqk_low[:, k]),
                              (lambda k: x_high[s][:, k], lambda k: x_low[s][:, k]), KC).then_inc(qk_done, 1)
                        before = None if first and s == 0 else (i - 1, NS - 1) if s == 0 else (i, s - 1)
                        for r in range(R):
                            px = slice(r * W, (r + 1) * W)
                            pe.wait_ge(bank_free[r], b * BANK_ALL + i * NS + s + 1)
                            between = (lambda at: row_score(*before, at)) if before and r == 0 else None
                            if between:
                                wait_row(*before)
                            last = three(bank4[:, r], (lambda k: x_high[s][:, k, px], lambda k: x_low[s][:, k, px]),
                                         (lambda k: wv_high[:, k], lambda k: wv_low[:, k]), KC, between)
                            last.then_inc(v_done, 1)

                groups(0, True)
                with pe.Fori(1, NI) as i:
                    groups(i, False)
                wait_row(NI - 1, NS - 1)
                for j in range(2 * R):
                    row_score(NI - 1, NS - 1, j)

                for u in range(NG):
                    s = u % S
                    pe.wait_ge(bank_free[s], b * BANK_ALL + BANK_PROJ + u // S + 1)
                    for r in range(R):
                        q, kh, kl = (t[:, u * R + r, :] for t in by_column)
                        dst = bank4[:, s, r * P:(r + 1) * P]
                        pe.matmul(dst, q, kh, start=True, stop=False)
                        pe.matmul(dst, q, kl, start=False, stop=False)
                        last = pe.matmul(dst, ident_b[:], far_b[:], start=False, stop=True)
                    last.then_inc(score_done, 1)
                    if more and u == MEANS_AT:
                        group_means(b + 1)
                    if more and u == SQUARES_AT:
                        group_variances(b + 1)

                for s in range(S):
                    pe.wait_ge(bank_free[s], b * BANK_ALL + BANK_PROJ + BANK_SCORE + 1)
                pe.wait_ge(row_exp_done, NG * (b + 1) + 1)
                pe.wait_ge(sums_done, (b + 1) * len(SHIFTED))
                pe.transpose(bank_s[:, 0:P], mx[1], ident_f[:])
                pe.transpose(bank_s[:, P:2 * P], zs[1], ident_f[:]).then_inc(join_pe, 1)

                def scores(d, u, r):
                    q, kh, kl = (t[:, u * UR + r, :] for t in (by_row, by_column)[d])
                    dst = unit_pair(d, u)[:, r // R, (r % R) * P:(r % R + 1) * P]
                    pe.matmul(dst, kh, q, start=True, stop=False)
                    pe.matmul(dst, kl, q, start=False, stop=False)
                    if d == 1:
                        pe.matmul(dst, ident_b[:], far_b[:], start=False, stop=False)
                    return dst

                pe.wait_ge(join_dve, b * JOIN_DVE + 8)
                pe.transpose(bank_s[:, 2 * P:3 * P], neg_l[1], ident_f[:]).then_inc(join_pe, 1)
                EARLY = 2
                pe.wait_ge(join_dve, b * JOIN_DVE + 13)
                for u in range(EARLY):
                    for r in range(UR):
                        dst, row = scores(1, u, r), u * UR + r
                        for part in range(3):
                            last = pe.matmul(dst, ident_b[:, row:row + 1].to_broadcast([P, P]),
                                             neg_l3[1][:, part, :], start=False, stop=(part == 2))
                    last.then_inc(logit_done, 1)

                for d in (1, 0):
                    pe.wait_ge(stack_in[d], (b + 1) * 3 * 16)
                    for u in range(EARLY if d == 1 else 0, UNITS):
                        shifts = l_stack[d][0:3 * BLK, u * UR // BLK, :]
                        if d == 0 or u >= PAIRS:
                            pe.wait_ge(exp_done[(u - PAIRS) % NS],
                                       (b * 2 + 1 - d) * (UNITS // NS) + (u - PAIRS) // NS + 2)
                        for r in range(UR):
                            dst = scores(d, u, r)
                            hot = (u * UR + r) % BLK
                            last = pe.matmul(dst, onehot_b[0:3 * BLK, hot:hot + 1].to_broadcast([3 * BLK, P]), shifts,
                                             start=False, stop=True)
                        last.then_inc(logit_done, 1)

                for s in range(NS):
                    pe.wait_ge(p_free[s], (b + 1) * 2 * (UNITS // NS) + 1)
                stand(pe, "pe")
                with pe.Fori(0, KC) as c:
                    for d in (1, 0):
                        probs = prob_row if d == 0 else prob_col
                        for u in range(NG):
                            s = u % S
                            t = wait_feed(pe, b * KC + c, "v", d, u)
                            pe.wait_ge(bank_free[s], b * BANK_ALL + BANK_PROJ + BANK_SCORE
                                       + (c * 2 + 1 - d) * NT + u // S + 1)
                            for r in range(R):
                                ph, pl = (probs[:, u * R + r, t2, :] for t2 in range(2))
                                last = three(bank4[:, s, r * P:(r + 1) * P],
                                             (lambda k: v_feed[t][:, r, 0], lambda k: v_feed[t][:, r, 1]),
                                             (lambda k: ph, lambda k: pl), 1)
                            last.then_inc(att_done[s], 1)

            group_means(0)
            group_variances(0)
            pe.sem_inc(qk_wide_ready, 1)
            pe.sem_inc(row_exp_done, 1)
            per_image(pe, image)

        @block.scalar
        def _(act):
            t = KC * C + KC * P
            act.dma_start(ident_f[:], ident).then_inc(const_in, 16)
            act.dma_start(group_f[:], group_mean).then_inc(const_in, 16)
            act.dma_start(b32[:, t:t + P], far_diag).then_inc(const_in, 16)
            act.dma_start(b32[:, t + P:t + P + BLK], onehot).then_inc(const_in, 16)
            act.dma_start(bqk_s, bqk.rearrange("(p a) -> p a", a=1)).then_inc(const_in, 16)
            act.dma_start(bv_s, bv).then_inc(const_in, 16)
            act.dma_start(b32[:, t + P + BLK:t + P + BLK + P], ident).then_inc(const_in, 16)
            for s in range(NS):
                act.sem_inc(v_stored[s], 16)
                act.sem_inc(p_free[s], 1)
            for s in range(S):
                act.sem_inc(acc_out[s], 16)

            def stat_logs(b):
                act.wait_ge(stat_dve, b * STAT_DVE + 7)
                nc.scalar.activation(small[:, 6, :], small[:, 5, :], ACT.Ln).then_inc(stat_act, 1)

            def stat_roots(b):
                act.wait_ge(stat_act, STAT_ACT * b + 1)
                nc.scalar.activation(small[:, 7, :], small[:, 6, :], ACT.Exp, scale=-0.5).then_inc(stat_act, 1)

            def image(b, more):
                for s in range(S):
                    act.wait_ge(acc_out[s], STORED * b * KC + 16)
                nc.scalar.activation(scratch1, bqk_s, ACT.Exp).then_inc(table_set, 1)
                act.wait_ge(table_set, 2 * b + 1)

                def row_exps(i, s):
                    act.wait_ge(row_negmax_ready, (b * NI + i) * NS + s + 1)
                    for r in range(R):
                        q = s * R + r
                        ins = nc.scalar.activation(exp_junk[q], bank_row[:, r * P:(r + 1) * P], ACT.Exp,
                                                   bias=row_neg_max[:, q:q + 1],
                                                   accum_out=lanes(zs[0], q, i * NS * R, 1))
                    ins.then_inc(row_exp_done, 1)

                def groups(i, first):
                    n = b * NI + i
                    for s in range(NS):
                        g = n * NS + s
                        before = None if first and s == 0 else (i - 1, NS - 1) if s == 0 else (i, s - 1)
                        act.wait_ge(qk_done, g + 1)
                        nc.scalar.activation(qk_wide, bank_qk, ACT.Identity, bias=bqk_s, scale=PROJ_DOWN
                                             ).then_inc(qk_wide_ready, 1)
                        act.wait_ge(v_stored[s], 16 * n + 16)
                        act.wait_ge(qk_split, g + 1)
                        rows = lanes_at((i * NS + s) * R, R)
                        act.dma_start(qk_rows[CQ:P, rows, 0, :],
                                      q_low_stage[s][0:CQ].rearrange("p (r w) -> p r w", r=R)
                                      ).then_inc(qk_moved[s], 16)
                        act.dma_start(qk_rows[0:CQ, rows, 1, :], qk_rows[CQ:P, rows, 1, :]).then_inc(qk_moved[s], 16)
                        act.dma_start(k_low[0:CQ, rows, :], k_low[CQ:P, rows, :]).then_inc(qk_moved[s], 16)
                        for r in range(R):
                            act.wait_ge(v_done, V_AHEAD + g * R + r + 1)
                            nc.scalar.activation(v_tile[s][:, r, :, 0, :],
                                                 bank4[:, r].rearrange("p (k c) -> p k c", k=KC),
                                                 ACT.Copy, scale=PROJ_DOWN).then_inc(vh_ready, 1)
                            if r == 0 and before:
                                row_exps(*before)
                        for r in range(R):
                            act.wait_ge(bank_free[r], b * BANK_ALL + i * NS + s + 2)
                        act.dma_start(v_dram[rows].rearrange("r k w c -> w (r k) c"),
                                      v_tile[s].rearrange("p r k t c -> p (r k) (t c)")).then_inc(v_stored[s], 16)

                groups(0, True)
                with act.Fori(1, NI) as i:
                    groups(i, False)
                row_exps(NI - 1, NS - 1)

                act.wait_ge(row_exp_done, NG * (b + 1) + 1)
                for u in range(NG):
                    s = u % S
                    if u in BIASED:
                        j = BIASED.index(u)
                        if j > 1:
                            act.wait_ge(bank_free[BIASED[j - 2] % S],
                                        b * BANK_ALL + BANK_PROJ + BIASED[j - 2] // S + 2)
                        act.wait_ge(negmax_ready, b * len(BIASED) + j + 1)
                        for r in range(R):
                            ins = nc.scalar.activation(exp_junk[j % 2 * R + r], bank4[:, s, r * P:(r + 1) * P],
                                                       ACT.Exp, bias=neg_max[:, s * R + r:s * R + r + 1],
                                                       accum_out=zs[1][:, u * R + r:u * R + r + 1])
                        ins.then_inc(bank_free[s], 1)
                    else:
                        act.wait_ge(bank_free[s], b * BANK_ALL + BANK_PROJ + u // S + 2)
                        tile = shifted[SHIFTED.index(u) % 2]
                        nc.scalar.activation(tile, tile, ACT.Exp).then_inc(exps_ready, 1)

                act.wait_ge(join_dve, b * JOIN_DVE + 3)
                nc.scalar.activation(grown, shift2, ACT.Exp).then_inc(join_act, 1)
                act.wait_ge(join_dve, b * JOIN_DVE + 6)
                nc.scalar.activation(log_z, z_all, ACT.Ln).then_inc(join_act, 1)
                if more:
                    stat_logs(b + 1)
                    stat_roots(b + 1)
                nc.scalar.activation(scratch1, bqk_s, ACT.Exp).then_inc(table_set, 1)
                act.wait_ge(table_set, 2 * b + 2)

                for s in range(NS):
                    act.wait_ge(v_stored[s], 16 * NI * (b + 1) + 16)
                for d in (1, 0):
                    probs = prob_col if d == 1 else prob_row
                    for u in range(UNITS):
                        s = u % NS
                        logits = unit_pair(d, u).rearrange("p a n -> p (a n)")
                        act.wait_ge(logit_done, (b * 2 + 1 - d) * UNITS + u + 1)
                        act.wait_ge(p_free[s], (b * 2 + 1 - d) * (UNITS // NS) + u // NS + 1)
                        if u % 2 == 1:
                            nc.scalar.activation(probs[:, u * UR:(u + 1) * UR, 0, :], logits.rearrange(
                                "p (r n) -> p r n", r=UR), ACT.Exp)
                        nc.scalar.activation(p_wide[s], logits, ACT.Exp).then_inc(exp_done[s], 1)

                for s in range(NS):
                    act.wait_ge(p_free[s], (b + 1) * 2 * (UNITS // NS) + 1)
                with act.Fori(0, KC) as c:
                    m = b * KC + c
                    nc.scalar.activation(bv_now, bv_s[:, bass.ds(c, 1)], ACT.Copy).then_inc(bias_set, 1)
                    act.wait_ge(bias_set, m + 1)
                    for s in range(S):
                        act.wait_ge(acc_out[s], STORED * m + 16)
                    for u in range(NG):
                        s = u % S
                        act.wait_ge(att_done[s], step_done(m, 1, u))
                        nc.scalar.activation(acc[:, :, u * R:(u + 1) * R],
                                             bank4[:, s].rearrange("p (r n) -> p n r", r=R), ACT.Identity,
                                             bias=bv_now, scale=ATT_DOWN).then_inc(bank_free[s], 1)
                    for u in range(NG):
                        s = u % S
                        act.wait_ge(bank_free[s], b * BANK_ALL + BANK_PROJ + BANK_SCORE + (c * 2 + 1) * NT + u // S + 2)
                        act.dma_start(out_chunk[b][c][:, u * R:(u + 1) * R, :], acc[:, u * R:(u + 1) * R, :]
                                      ).then_inc(acc_out[s], 16)

            stat_logs(0)
            stat_roots(0)
            per_image(act, image)
            for s in range(S):
                act.wait_ge(acc_out[s], STORED * NB * KC + 16)

        @block.vector
        def _(dve):
            for s in range(NS):
                dve.sem_inc(stat_free[s], 1)
            for j in range(FIRST):
                dve.sem_inc(first_free[j], 1)
            for s in range(NS):
                dve.sem_inc(qk_moved[s], MOVE)

            dve.wait_ge(const_in, CONSTS)
            wide = b32[:, 0:KC * C + KC * P]
            nc.vector.tensor_scalar(wide, wide, W_SCALE, None, ALU.mult).then_inc(w_split, 1)
            dve.wait_ge(w_split, 1)
            wv_wide, wqk_wide = b32[:, 0:KC * C], b32[:, KC * C:KC * C + KC * P]
            wvh, wvl = region_w[:, 0:KC * C], region_w[:, KC * C:2 * KC * C]
            o = 2 * KC * C
            wqh, wql = region_w[:, o:o + KC * P], region_w[:, o + KC * P:o + 2 * KC * P]
            t = KC * C + KC * P
            nc.vector.tensor_copy(far_b[:], b32[:, t:t + P])
            nc.vector.tensor_copy(onehot_b[:], b32[:, t + P:t + P + BLK])
            nc.vector.tensor_copy(ident_b[:], b32[:, t + P + BLK:t + P + BLK + P])
            nc.vector.tensor_copy(wvh, wv_wide)
            nc.vector.tensor_copy(wqh, wqk_wide).then_inc(w_split, 1)
            dve.wait_ge(w_split, 2)
            nc.vector.tensor_tensor(wvl, wv_wide, wvh, ALU.subtract)
            nc.vector.tensor_tensor(wql, wqk_wide, wqh, ALU.subtract).then_inc(w_split, 1)

            def stat_group(b, i, s):
                dve.wait_ge(stat_in[s], 16 * (b * NI + i) + 16)
                for k in range(KC):
                    last = nc.vector.bn_stats(bn[:, k, lanes_at(i * NS + s, 1), :].rearrange("p a s -> p (a s)"),
                                              stat_tile[s][:, k])
                last.then_inc(stat_free[s], 1)

            def stat_link(b, count, ins):
                ins.then_inc(stat_dve, 1)
                dve.wait_ge(stat_dve, b * STAT_DVE + count)

            mean, mean_g, dev, dev2, mom, var_g, log_var, y = (small[:, j, :] for j in range(8))
            mean_var = small[:, 8:10, :].rearrange("p a k -> p (a k)")

            def stat_means(b):
                for k in range(KC):
                    last = nc.vector.bn_aggr(mean_var[:, 2 * k:2 * k + 2], bn[:, k].rearrange("p g s -> p (g s)"))
                stat_link(b, 1, last)
                stat_link(b, 2, nc.vector.tensor_copy(mean, mean_var.rearrange("p (k t) -> p t k", t=2)[:, 0, :]))

            def stat_moments(b):
                dve.wait_ge(stat_pe, STAT_PE * b + 1)
                stat_link(b, 3, nc.vector.tensor_copy(mean_g, bank_s[:, 3 * P:3 * P + KC]))
                stat_link(b, 4, nc.vector.tensor_tensor(dev, mean, mean_g, ALU.subtract))
                stat_link(b, 5, nc.vector.tensor_tensor(dev2, dev, dev, ALU.mult))
                var = mean_var.rearrange("p (k t) -> p t k", t=2)[:, 1, :]
                stat_link(b, 6, nc.vector.tensor_tensor(mom, dev2, var, ALU.add))

            def stat_variances(b):
                dve.wait_ge(stat_pe, STAT_PE * b + 2)
                stat_link(b, 7, nc.vector.tensor_scalar(var_g, bank_s[:, 3 * P + KC:3 * P + 2 * KC], EPS, None, ALU.add))

            def stat_scales(b):
                dve.wait_ge(stat_act, STAT_ACT * b + 2)
                stat_link(b, 8, nc.vector.tensor_tensor(dev, y, y, ALU.mult))
                stat_link(b, 9, nc.vector.tensor_tensor(dev2, dev, var_g, ALU.mult))
                stat_link(b, 10, nc.vector.tensor_scalar(dev, dev2, -0.5, 1.5, ALU.mult, ALU.add))
                stat_link(b, 11, nc.vector.tensor_tensor(dev2, y, dev, ALU.mult))
                stat_link(b, 12, nc.vector.tensor_scalar(norm_scale, dev2, X_SCALE, None, ALU.mult))
                stat_link(b, 13, nc.vector.scalar_tensor_tensor(out=norm_bias, in0=mean_g, scalar=-1.0, in1=norm_scale,
                                                                op0=ALU.mult, op1=ALU.mult))
                stand(dve, "dve")

            def image(b, more):
                dve.wait_ge(x_in[0], 16 * b * NI + 16)
                dve.wait_ge(v_done, b * NG * R + R)
                stand(dve, "dve")
                for k in range(KC):
                    nc.vector.tensor_scalar(x_high[0][:, k], x_tile[0][:, k], norm_scale[:, k:k + 1],
                                            norm_bias[:, k:k + 1], ALU.mult, ALU.add).then_inc(first_parts, 1)
                dve.wait_ge(first_parts, (2 * b + 1) * KC)
                for k in range(KC):
                    nc.vector.tensor_scalar(x_tile[0][:, k], x_tile[0][:, k], norm_scale[:, k:k + 1],
                                            norm_bias[:, k:k + 1], ALU.mult, ALU.add).then_inc(first_parts, 1)
                dve.wait_ge(first_parts, (2 * b + 2) * KC)
                nc.vector.tensor_tensor(x_low[0], x_tile[0], x_high[0], ALU.subtract).then_inc(parts_ready[0], 1)
                for s in range(S):
                    dve.wait_ge(acc_out[s], STORED * b * KC + 16)
                stand(dve, "dve")

                def row_tops(i, s):
                    g = (b * NI + i) * NS + s
                    tops = lanes(mx[0], s * R, i * NS * R, R)
                    dve.wait_ge(row_score_done, g + 1)
                    nc.vector.tensor_reduce(tops, bank_row.rearrange("p (r n) -> p r n", r=R),
                                            AXX, ALU.max).then_inc(row_max_ready, 1)
                    dve.wait_ge(row_max_ready, g + 1)
                    dve.wait_ge(row_exp_done, g + 1)
                    nc.vector.tensor_scalar(row_neg_max[:, s * R:(s + 1) * R], tops, -1.0, None,
                                            ALU.mult).then_inc(row_negmax_ready, 1)

                def groups(i, first):
                    n = b * NI + i
                    for s in range(NS):
                        g = n * NS + s
                        before = None if first and s == 0 else (i - 1, NS - 1) if s == 0 else (i, s - 1)
                        rows = lanes_at((i * NS + s) * R, R)
                        wide_q = qk_wide[0:CQ].rearrange("p (r w) -> p r w", r=R)
                        wide_k = qk_wide[CQ:P].rearrange("p (r w) -> p r w", r=R)
                        dve.wait_ge(qk_moved[s], MOVE * n + MOVE)
                        dve.wait_ge(qk_wide_ready, g + 2)
                        nc.vector.tensor_copy(qk_rows[0:CQ, rows, 0, :], wide_q).then_inc(qh_ready, 1)
                        nc.vector.tensor_copy(qk_rows[CQ:P, rows, 1, :], wide_k).then_inc(qh_ready, 1)
                        dve.wait_ge(qh_ready, 2 * g + 2)
                        nc.vector.tensor_tensor(q_low_stage[s][0:CQ].rearrange("p (r w) -> p r w", r=R), wide_q,
                                                qk_rows[0:CQ, rows, 0, :], ALU.subtract)
                        nc.vector.tensor_tensor(k_low[CQ:P, rows, :], wide_k, qk_rows[CQ:P, rows, 1, :],
                                                ALU.subtract).then_inc(qk_split, 1)
                        for r in range(R):
                            dve.wait_ge(vh_ready, g * R + r + 1)
                            bank = bank4[:, r].rearrange("p (k c) -> p k c", k=KC)
                            nc.vector.scalar_tensor_tensor(out=v_tile[s][:, r, :, 1, :], in0=bank, scalar=PROJ_DOWN,
                                                           in1=v_tile[s][:, r, :, 0, :], op0=ALU.mult,
                                                           op1=ALU.subtract).then_inc(bank_free[r], 1)
                            if r == 0 and before:
                                row_tops(*before)
                        if more:
                            stat_group(b, i, s)

                groups(0, True)
                with dve.Fori(1, NI) as i:
                    groups(i, False)
                row_tops(NI - 1, NS - 1)
                if more:
                    for s in range(NS):
                        dve.wait_ge(stat_free[s], (b + 1) * NI + 1)
                    stand(dve, "dve")

                def shifted_sum(j):
                    dve.wait_ge(exps_ready, b * len(SHIFTED) + j + 1)
                    nc.vector.tensor_reduce(zs[1][:, SHIFTED[j] * R:(SHIFTED[j] + 1) * R],
                                            shifted[j % 2].rearrange("p (r n) -> p r n", r=R),
                                            AXX, ALU.add).then_inc(sums_done, 1)

                for u in range(NG):
                    s = u % S
                    scores = bank4[:, s].rearrange("p (r n) -> p r n", r=R)
                    tops = mx[1][:, u * R:(u + 1) * R]
                    dve.wait_ge(score_done, b * NG + u + 1)
                    nc.vector.tensor_reduce(tops, scores, AXX, ALU.max).then_inc(max_ready, 1)
                    dve.wait_ge(max_ready, b * NG + u + 1)
                    if u in BIASED:
                        nc.vector.tensor_scalar(neg_max[:, s * R:(s + 1) * R], tops, -1.0, None,
                                                ALU.mult).then_inc(negmax_ready, 1)
                    else:
                        j = SHIFTED.index(u)
                        nc.vector.tensor_tensor(shifted[j % 2].rearrange("p (r n) -> p r n", r=R), scores,
                                                tops.unsqueeze(2).broadcast_to([P, R, P]),
                                                ALU.subtract).then_inc(bank_free[s], 1)
                        if j > 0:
                            shifted_sum(j - 1)
                    if more and u == 1:
                        stat_means(b + 1)
                    if more and u == MOMENTS_AT:
                        stat_moments(b + 1)
                    if more and u == VARIANCES_AT:
                        stat_variances(b + 1)
                shifted_sum(len(SHIFTED) - 1)
                dve.wait_ge(sums_done, (b + 1) * len(SHIFTED))

                stand(dve, "dve")

                count = [0]

                def link(ins):
                    ins.then_inc(join_dve, 1)
                    count[0] += 1
                    dve.wait_ge(join_dve, b * JOIN_DVE + count[0])

                def split3(d):
                    link(nc.vector.tensor_copy(neg_l3[d][:, 0, :], neg_l[d]))
                    link(nc.vector.tensor_tensor(rest, neg_l[d], neg_l3[d][:, 0, :], ALU.subtract))
                    link(nc.vector.tensor_copy(neg_l3[d][:, 1, :], rest))
                    link(nc.vector.tensor_tensor(rest, rest, neg_l3[d][:, 1, :], ALU.subtract))
                    link(nc.vector.tensor_copy(neg_l3[d][:, 2, :], rest))

                dve.wait_ge(join_pe, b * JOIN_PE + 1)
                link(nc.vector.tensor_tensor(m_all, bank_s[:, 0:P], mx[0], ALU.max))
                link(nc.vector.tensor_tensor(shift2[:, 0:P], bank_s[:, 0:P], m_all, ALU.subtract))
                link(nc.vector.tensor_tensor(shift2[:, P:2 * P], mx[0], m_all, ALU.subtract))
                dve.wait_ge(join_act, b * JOIN_ACT + 1)
                link(nc.vector.tensor_tensor(z_all, bank_s[:, P:2 * P], grown[:, 0:P], ALU.mult))
                link(nc.vector.tensor_tensor(rest, zs[0], grown[:, P:2 * P], ALU.mult))
                link(nc.vector.tensor_tensor(z_all, z_all, rest, ALU.add))
                dve.wait_ge(join_act, b * JOIN_ACT + 2)
                link(nc.vector.tensor_tensor(rest, m_all, log_z, ALU.add))
                link(nc.vector.tensor_scalar(neg_l[1], rest, -1.0, P_SCALE_LOG2 * log(2.0),
                                             ALU.mult, ALU.add))
                split3(1)
                dve.wait_ge(join_pe, b * JOIN_PE + 2)
                link(nc.vector.tensor_copy(neg_l[0], bank_s[:, 2 * P:3 * P]))
                split3(0)
                assert count[0] == JOIN_DVE

                for s in range(NS):
                    dve.wait_ge(v_stored[s], 16 * NI * (b + 1) + 16)
                stand(dve, "dve")
                for d in (1, 0):
                    probs = prob_col if d == 1 else prob_row
                    for u in range(UNITS):
                        s = u % NS
                        high, low = (probs[:, u * UR:(u + 1) * UR, t, :] for t in range(2))
                        src = p_wide[s].rearrange("p (r n) -> p r n", r=UR)
                        dve.wait_ge(exp_done[s], (b * 2 + 1 - d) * (UNITS // NS) + u // NS + 2)
                        if u % 2 == 0:
                            nc.vector.tensor_copy(high, src).then_inc(ph_ready, 1)
                            dve.wait_ge(ph_ready, (b * 2 + 1 - d) * (UNITS // 2) + u // 2 + 1)
                        nc.vector.tensor_tensor(low, src, high, ALU.subtract).then_inc(p_free[s], 1)

                if more:
                    stat_scales(b + 1)

                with dve.Fori(0, KC) as c:
                    m = b * KC + c
                    for u in range(NG):
                        s = u % S
                        dve.wait_ge(x_added, (m + 1) * NG + u + 1)
                        dve.wait_ge(att_done[s], step_done(m, 0, u))
                        part = acc[:, u * R:(u + 1) * R, :]
                        nc.vector.scalar_tensor_tensor(out=part, in0=bank4[:, s].rearrange("p (r n) -> p r n", r=R),
                                                       scalar=ATT_DOWN, in1=part,
                                                       op0=ALU.mult, op1=ALU.add).then_inc(bank_free[s], 1)

            with dve.Fori(0, NI // FIRST) as i:
                for j in range(FIRST):
                    dve.wait_ge(first_in[j], 16 * i + 16)
                    for half in range(2):
                        for k in range(KC):
                            last = nc.vector.bn_stats(
                                bn[:, k, j * 2 + half:, :][:, bass.ds(i * FIRST * 2, 1), :].rearrange("p a s -> p (a s)"),
                                first_tile[j][:, k, half * PIX:(half + 1) * PIX])
                    last.then_inc(first_free[j], 1)
            for j in range(FIRST):
                dve.wait_ge(first_free[j], NI // FIRST + 1)
            for step in (stat_means, stat_moments, stat_variances, stat_scales):
                step(0)
            per_image(dve, image)


_OUT = "out_dram"


def kernel(x, L0_conv_Wq, L0_conv_bq, L0_conv_Wk, L0_conv_bk, L0_conv_Wv, L0_conv_bv):
    import numpy as np
    import concourse.bacc as bacc
    from concourse.bass_utils import run_bass_kernel_spmd

    G = 16
    B, C, H, W = x.shape
    rows = np.arange(128)
    arrays = {
        "x_dram": np.ascontiguousarray(x),
        "wv_t_dram": np.ascontiguousarray(np.asarray(L0_conv_Wv).T),
        "wqk_t_dram": np.ascontiguousarray(np.concatenate([L0_conv_Wq, L0_conv_Wk], 0).T),
        "bqk_dram": np.concatenate([L0_conv_bq, L0_conv_bk]),
        "bv_dram": np.ascontiguousarray(np.asarray(L0_conv_bv).reshape(C // 128, 128).T),
        "ident_dram": np.eye(128, dtype=np.float32),
        "group_mean_dram": (rows[:, None] // G == rows[None] // G).astype(np.float32) / np.float32(G),
        "onehot_dram": (rows[:, None] % 32 == np.arange(32)[None]).astype(np.float32),
        "far_diag_dram": np.where(np.eye(128, dtype=bool), np.float32(FAR), np.float32(0)).astype(np.float32),
    }
    nc = bacc.Bacc("TRN2", target_bir_lowering=False, num_devices=1)
    args = [nc.dram_tensor(n, a.shape, mybir.dt.from_np(a.dtype), kind="ExternalInput").ap()
            for n, a in arrays.items()]
    args.append(nc.dram_tensor(_OUT, (B, C, H, W), F32, kind="ExternalOutput").ap())
    criss_cross_program(nc, *args)
    r = run_bass_kernel_spmd(nc, [arrays], core_ids=[0])
    return r.results[0][_OUT]
```
